# Optimizing a Trainium2 kernel written in Bass

```python
import numpy as np
import jax
import jax.numpy as jnp

def _softmax(x, axis=-1):
    return jax.nn.softmax(x, axis=axis)

def _gelu(x):
    return jax.nn.gelu(x, approximate=True)

def _silu(x):
    return jax.nn.silu(x)

def _sigmoid(x):
    return jax.nn.sigmoid(x)

def _layernorm(x, axis=-1, eps=1e-05):
    m = jnp.mean(x, axis=axis, keepdims=True)
    v = jnp.var(x, axis=axis, keepdims=True)
    return (x - m) / jnp.sqrt(v + eps)

def _scatter_add(tgt, idx, src, axis=0):
    return tgt.at[idx].add(src)

def _segment_sum(src, seg, n):
    return jax.ops.segment_sum(src, seg, n)
kernel_name = 'mk_pixart_seq_d2_seqx_r2_33bc91'

def setup_inputs(seed: int=0):
    np.random.seed(seed)
    _w = jnp.asarray

    def _rec_inputs():
        import jax
        import jax.numpy as jnp
        _rk = jax.random.key(seed)
        x = -0.0003929 + 0.9999 * jax.random.normal(jax.random.fold_in(_rk, 1), (8, 512, 512), jnp.float32)
        _lenS = 512 - jax.random.randint(jax.random.fold_in(_rk, 7), (8,), 0, max(1, 512 // 4) + 1, jnp.int32)
        _lenS2 = 77 - jax.random.randint(jax.random.fold_in(_rk, 8), (8,), 0, max(1, 77 // 4) + 1, jnp.int32)
        _ctx_1024P = jax.random.normal(jax.random.fold_in(_rk, 11), (8, 16, 512), jnp.float32)
        _ctx_1024c = jax.random.dirichlet(jax.random.fold_in(_rk, 511), 0.3 * jnp.ones((16,), jnp.float32), (8, 77))
        _ctx_1024t = jnp.einsum('bsk,bkd->bsd', _ctx_1024c, _ctx_1024P)
        _ctx_1024t = _ctx_1024t * jax.lax.rsqrt(jnp.mean(jnp.square(_ctx_1024t)) + 1e-12) * 0.953939
        ctx_1024 = -1.39393e-06 + 0.999914 * (_ctx_1024t + 0.3 * jax.random.normal(jax.random.fold_in(_rk, 611), (8, 77, 512), jnp.float32))
        cond_1024 = -0.00920427 + 1.00102 * jax.random.normal(jax.random.fold_in(_rk, 12), (8, 512), jnp.float32)
        return (x, ctx_1024, cond_1024)
    x, ctx_1024, cond_1024 = _rec_inputs()

    def _L0_xcond_setup():
        import jax, jax.numpy as jnp
        import numpy as np
        EPS = 1e-05

        def _ada_ln(x, c, W_ss, b_ss):
            mu = jnp.mean(x, axis=-1, keepdims=True)
            var = jnp.mean((x - mu) ** 2, axis=-1, keepdims=True)
            h = (x - mu) / jnp.sqrt(var + EPS)
            ss = jax.nn.silu(c) @ W_ss + b_ss
            scale, bias = jnp.split(ss, 2, axis=-1)
            return (1.0 + scale)[:, None, :] * h + bias[:, None, :]
        key = jax.random.key(seed)
        ks = jax.random.split(key, 12)
        B, Lq, Lkv, H = (8, 1024, 256, 512)
        s = 0.02
        return {'x_q': jax.random.normal(ks[0], (B, Lq, H), jnp.float32), 'x_kv': jax.random.normal(ks[1], (B, Lkv, H), jnp.float32), 't_vec': jax.random.normal(ks[2], (B, H), jnp.float32), 'Wq': jax.random.normal(ks[3], (H, H), jnp.float32) * s, 'bq': jnp.zeros((H,), jnp.float32), 'Wkv': jax.random.normal(ks[4], (H, 2 * H), jnp.float32) * s, 'bkv': jnp.zeros((2 * H,), jnp.float32), 'Wp': jax.random.normal(ks[5], (H, H), jnp.float32) * s, 'bp': jnp.zeros((H,), jnp.float32), 'Wss_q': jax.random.normal(ks[6], (H, 2 * H), jnp.float32) * s, 'bss_q': jnp.zeros((2 * H,), jnp.float32), 'Wss_kv': jax.random.normal(ks[7], (H, 2 * H), jnp.float32) * s, 'bss_kv': jnp.zeros((2 * H,), jnp.float32)}
    _L0_xcond_all = _L0_xcond_setup()
    _L0_xcond_in = {k: v for k, v in _L0_xcond_all.items() if k in ('Wq', 'bq', 'Wkv', 'bkv', 'Wp', 'bp', 'Wss_q', 'bss_q', 'Wss_kv', 'bss_kv')}
    del _L0_xcond_all

    def _L1_xcond_setup():
        import jax, jax.numpy as jnp
        import numpy as np
        LN_EPS = 1e-06

        def _ln(x):
            mu = jnp.mean(x, axis=-1, keepdims=True)
            var = jnp.var(x, axis=-1, keepdims=True)
            return (x - mu) * jax.lax.rsqrt(var + LN_EPS)
        key = jax.random.key(seed)
        H, NH = (512, 16)
        B, N, S = (4, 512, 77)
        MLP = int(H * 4.0)
        ks = jax.random.split(key, 20)
        s = 1.0 / np.sqrt(H)
        return {'x': jax.random.normal(ks[0], (B, N, H), jnp.float32), 'c': jax.random.normal(ks[1], (B, H), jnp.float32), 'context': jax.random.normal(ks[2], (B, S, H), jnp.float32), 'W_mod': jax.random.normal(ks[3], (H, 6 * H), jnp.float32) * s, 'b_mod': jnp.zeros((6 * H,), jnp.float32), 'W_qkv': jax.random.normal(ks[4], (H, 3 * H), jnp.float32) * s, 'b_qkv': jnp.zeros((3 * H,), jnp.float32), 'W_proj': jax.random.normal(ks[5], (H, H), jnp.float32) * s, 'b_proj': jnp.zeros((H,), jnp.float32), 'W_qc': jax.random.normal(ks[6], (H, H), jnp.float32) * s, 'b_qc': jnp.zeros((H,), jnp.float32), 'W_kvc': jax.random.normal(ks[7], (H, 2 * H), jnp.float32) * s, 'b_kvc': jnp.zeros((2 * H,), jnp.float32), 'W_cproj': jax.random.normal(ks[8], (H, H), jnp.float32) * s, 'b_cproj': jnp.zeros((H,), jnp.float32), 'W_mlp1': jax.random.normal(ks[9], (H, MLP), jnp.float32) * s, 'b_mlp1': jnp.zeros((MLP,), jnp.float32), 'W_mlp2': jax.random.normal(ks[10], (MLP, H), jnp.float32) * (1.0 / np.sqrt(MLP)), 'b_mlp2': jnp.zeros((H,), jnp.float32)}
    _L1_xcond_all = _L1_xcond_setup()
    _L1_xcond_in = {k: v for k, v in _L1_xcond_all.items() if k in ('W_mod', 'b_mod', 'W_qkv', 'b_qkv', 'W_proj', 'b_proj', 'W_qc', 'b_qc', 'W_kvc', 'b_kvc', 'W_cproj', 'b_cproj', 'W_mlp1', 'b_mlp1', 'W_mlp2', 'b_mlp2')}
    del _L1_xcond_all
    return {'x': x, 'ctx_1024': ctx_1024, 'cond_1024': cond_1024, 'L0_xcond_Wq': _L0_xcond_in['Wq'], 'L0_xcond_bq': _L0_xcond_in['bq'], 'L0_xcond_Wkv': _L0_xcond_in['Wkv'], 'L0_xcond_bkv': _L0_xcond_in['bkv'], 'L0_xcond_Wp': _L0_xcond_in['Wp'], 'L0_xcond_bp': _L0_xcond_in['bp'], 'L0_xcond_Wss_q': _L0_xcond_in['Wss_q'], 'L0_xcond_bss_q': _L0_xcond_in['bss_q'], 'L0_xcond_Wss_kv': _L0_xcond_in['Wss_kv'], 'L0_xcond_bss_kv': _L0_xcond_in['bss_kv'], 'L1_xcond_W_mod': _L1_xcond_in['W_mod'], 'L1_xcond_b_mod': _L1_xcond_in['b_mod'], 'L1_xcond_W_qkv': _L1_xcond_in['W_qkv'], 'L1_xcond_b_qkv': _L1_xcond_in['b_qkv'], 'L1_xcond_W_proj': _L1_xcond_in['W_proj'], 'L1_xcond_b_proj': _L1_xcond_in['b_proj'], 'L1_xcond_W_qc': _L1_xcond_in['W_qc'], 'L1_xcond_b_qc': _L1_xcond_in['b_qc'], 'L1_xcond_W_kvc': _L1_xcond_in['W_kvc'], 'L1_xcond_b_kvc': _L1_xcond_in['b_kvc'], 'L1_xcond_W_cproj': _L1_xcond_in['W_cproj'], 'L1_xcond_b_cproj': _L1_xcond_in['b_cproj'], 'L1_xcond_W_mlp1': _L1_xcond_in['W_mlp1'], 'L1_xcond_b_mlp1': _L1_xcond_in['b_mlp1'], 'L1_xcond_W_mlp2': _L1_xcond_in['W_mlp2'], 'L1_xcond_b_mlp2': _L1_xcond_in['b_mlp2']}

def reference(x, ctx_1024, cond_1024, L0_xcond_Wq, L0_xcond_bq, L0_xcond_Wkv, L0_xcond_bkv, L0_xcond_Wp, L0_xcond_bp, L0_xcond_Wss_q, L0_xcond_bss_q, L0_xcond_Wss_kv, L0_xcond_bss_kv, L1_xcond_W_mod, L1_xcond_b_mod, L1_xcond_W_qkv, L1_xcond_b_qkv, L1_xcond_W_proj, L1_xcond_b_proj, L1_xcond_W_qc, L1_xcond_b_qc, L1_xcond_W_kvc, L1_xcond_b_kvc, L1_xcond_W_cproj, L1_xcond_b_cproj, L1_xcond_W_mlp1, L1_xcond_b_mlp1, L1_xcond_W_mlp2, L1_xcond_b_mlp2):
    import jax
    import jax.numpy as jnp

    def _L0_xcond_ref(x_q, x_kv, t_vec, Wq, bq, Wkv, bkv, Wp, bp, Wss_q, bss_q, Wss_kv, bss_kv):
        import jax, jax.numpy as jnp
        import numpy as np
        EPS = 1e-05

        def _ada_ln(x, c, W_ss, b_ss):
            mu = jnp.mean(x, axis=-1, keepdims=True)
            var = jnp.mean((x - mu) ** 2, axis=-1, keepdims=True)
            h = (x - mu) / jnp.sqrt(var + EPS)
            ss = jax.nn.silu(c) @ W_ss + b_ss
            scale, bias = jnp.split(ss, 2, axis=-1)
            return (1.0 + scale)[:, None, :] * h + bias[:, None, :]
        B, Lq, H = x_q.shape
        Lkv = x_kv.shape[1]
        nh = 16
        dh = H // nh
        xq = _ada_ln(x_q, t_vec, Wss_q, bss_q)
        xkv = _ada_ln(x_kv, t_vec, Wss_kv, bss_kv)
        q = (xq @ Wq + bq).reshape(B, Lq, nh, dh)
        kv = (xkv @ Wkv + bkv).reshape(B, Lkv, 2, nh, dh)
        k = kv[:, :, 0]
        v = kv[:, :, 1]
        scores = jnp.einsum('bqhd,bkhd->bhqk', q, k) / jnp.sqrt(jnp.float32(dh))
        attn = jax.nn.softmax(scores, axis=-1)
        out = jnp.einsum('bhqk,bkhd->bqhd', attn, v).reshape(B, Lq, H)
        return x_q + (out @ Wp + bp)

    def _L1_xcond_ref(x, c, context, W_mod, b_mod, W_qkv, b_qkv, W_proj, b_proj, W_qc, b_qc, W_kvc, b_kvc, W_cproj, b_cproj, W_mlp1, b_mlp1, W_mlp2, b_mlp2):
        import jax, jax.numpy as jnp
        import numpy as np
        LN_EPS = 1e-06

        def _ln(x):
            mu = jnp.mean(x, axis=-1, keepdims=True)
            var = jnp.var(x, axis=-1, keepdims=True)
            return (x - mu) * jax.lax.rsqrt(var + LN_EPS)
        B, N, H = x.shape
        NH = 16
        hd = H // NH
        scale = hd ** (-0.5)
        c_proj = jax.nn.silu(c) @ W_mod + b_mod
        shift_a, scale_a, gate_a, shift_m, scale_m, gate_m = jnp.split(c_proj, 6, axis=-1)

        def modulate(t, shift, sc):
            return t * (1 + sc[:, None]) + shift[:, None]
        x_norm = modulate(_ln(x), shift_a, scale_a)
        qkv = x_norm @ W_qkv + b_qkv
        q, k, v = jnp.split(qkv, 3, axis=-1)
        q = q.reshape(B, N, NH, hd).transpose(0, 2, 1, 3)
        k = k.reshape(B, N, NH, hd).transpose(0, 2, 1, 3)
        v = v.reshape(B, N, NH, hd).transpose(0, 2, 1, 3)
        attn_w = jax.nn.softmax(jnp.einsum('bhqd,bhkd->bhqk', q, k) * scale, axis=-1)
        attn_out = jnp.einsum('bhqk,bhkd->bhqd', attn_w, v)
        attn_out = attn_out.transpose(0, 2, 1, 3).reshape(B, N, H)
        attn_out = attn_out @ W_proj + b_proj
        x = x + gate_a[:, None] * attn_out
        S = context.shape[1]
        q_c = _ln(x) @ W_qc + b_qc
        kv_c = _ln(context) @ W_kvc + b_kvc
        k_c, v_c = jnp.split(kv_c, 2, axis=-1)
        q_c = q_c.reshape(B, N, NH, hd).transpose(0, 2, 1, 3)
        k_c = k_c.reshape(B, S, NH, hd).transpose(0, 2, 1, 3)
        v_c = v_c.reshape(B, S, NH, hd).transpose(0, 2, 1, 3)
        c_attn_w = jax.nn.softmax(jnp.einsum('bhqd,bhsd->bhqs', q_c, k_c) * scale, axis=-1)
        c_attn_out = jnp.einsum('bhqs,bhsd->bhqd', c_attn_w, v_c)
        c_attn_out = c_attn_out.transpose(0, 2, 1, 3).reshape(B, N, H)
        c_attn_out = c_attn_out @ W_cproj + b_cproj
        x = x + c_attn_out
        x_norm2 = modulate(_ln(x), shift_m, scale_m)
        h = jax.nn.gelu(x_norm2 @ W_mlp1 + b_mlp1)
        h = h @ W_mlp2 + b_mlp2
        x = x + gate_m[:, None] * h
        return x
    x = _L0_xcond_ref(x, ctx_1024, cond_1024, L0_xcond_Wq, L0_xcond_bq, L0_xcond_Wkv, L0_xcond_bkv, L0_xcond_Wp, L0_xcond_bp, L0_xcond_Wss_q, L0_xcond_bss_q, L0_xcond_Wss_kv, L0_xcond_bss_kv)
    x = _L1_xcond_ref(x, cond_1024, ctx_1024, L1_xcond_W_mod, L1_xcond_b_mod, L1_xcond_W_qkv, L1_xcond_b_qkv, L1_xcond_W_proj, L1_xcond_b_proj, L1_xcond_W_qc, L1_xcond_b_qc, L1_xcond_W_kvc, L1_xcond_b_kvc, L1_xcond_W_cproj, L1_xcond_b_cproj, L1_xcond_W_mlp1, L1_xcond_b_mlp1, L1_xcond_W_mlp2, L1_xcond_b_mlp2)
    return x

_drawn_inputs = setup_inputs


def setup_inputs(seed=0):
    import zlib

    import numpy as np

    out = dict(_drawn_inputs(seed))
    spreads = {'L0_xcond_bq': (0.0, 2.0),
     'L0_xcond_bkv': (0.0, 0.1),
     'L0_xcond_bp': (0.0, 0.1),
     'L0_xcond_bss_q': (0.0, 0.8),
     'L0_xcond_bss_kv': (0.0, 0.338),
     'L1_xcond_b_mod': (0.0, 0.1),
     'L1_xcond_b_qkv': (0.0, 0.1),
     'L1_xcond_b_proj': (0.0, 0.1),
     'L1_xcond_b_qc': (0.0, 0.51),
     'L1_xcond_b_kvc': (0.0, 0.1),
     'L1_xcond_b_cproj': (0.0, 0.1),
     'L1_xcond_b_mlp1': (0.0, 0.1),
     'L1_xcond_b_mlp2': (0.0, 0.1)}
    factors = {'L0_xcond_Wq': 7.39, 'L0_xcond_Wss_q': 8.0}
    for name, (base, spread) in spreads.items():
        noise = np.random.default_rng([zlib.crc32(name.encode()), seed]).standard_normal(out[name].shape)
        drawn = base * np.exp(spread * noise) if base else spread * noise
        out[name] = jnp.asarray(drawn.astype(out[name].dtype))
    for name, factor in factors.items():
        out[name] = (out[name] * factor).astype(out[name].dtype)
    return out
```

```python
from contextlib import ExitStack

import numpy as np

import concourse.bass as bass
from concourse import mybir

F32 = mybir.dt.float32
F32R = mybir.dt.float32r
ALU = mybir.AluOpType
ACT = mybir.ActivationFunctionType
AX_X = mybir.AxisListType.X

P = 128
B, N, D = 8, 512, 512
S = 77
NH, HD = 16, 32
GH = P // HD
G = NH // GH
KC = D // P
NT = N // P
HID = 4 * D
SCALE = float(HD) ** -0.5
ST = 3 * HD
ST_MAX = ST + 2
SP_ = S + 1


class Tick:

    def __init__(self, sem, value):
        self.sem, self.value = sem, value


class Count:

    def __init__(self, sem):
        self.sem, self.value = sem, 0

    def next(self, by):
        self.value += by
        return Tick(self.sem, self.value)


class Lane:

    def __init__(self):
        self.queue, self.waited = [], {}

    def wait(self, *ticks):
        for t in ticks:
            if t is not None and self.waited.get(id(t.sem), 0) < t.value:
                self.waited[id(t.sem)] = t.value
                self.queue.append(lambda e, t=t: e.wait_ge(t.sem, t.value))

    def do(self, make, signal=None, by=1):
        tick = signal.next(by) if signal is not None else None
        if tick is None:
            self.queue.append(make)
        else:
            self.queue.append(lambda e: make(e).then_inc(tick.sem, by))
        return tick

    def emit(self, engine):
        for make in self.queue:
            make(engine)
        self.queue = []


class Ring:

    def __init__(self, slots):
        self.slots, self.freed, self.turn = list(slots), [()] * len(slots), 0

    def take(self, *writers):
        i = self.turn % len(self.slots)
        self.turn += 1
        for lane in writers:
            lane.wait(*self.freed[i])
        return i, self.slots[i]

    def free(self, i, *ticks):
        self.freed[i] = ticks


def build(nc, a, out):
    with ExitStack() as program:
        _build(nc, a, out, program)


def _build(nc, a, out, program):
    def dram(name, shape):
        return nc.dram_tensor(name, shape, F32, kind="Internal").ap()

    x1, x2, x3 = (dram(f"x{i}", (B, N, D)) for i in (1, 2, 3))
    q_parts = {s: dram(f"q_parts_{s}", (B, G, 2, P, N)) for s in ("L0", "self", "cross")}
    k_self = dram("k_parts_self", (B, G, 2, P, N))
    v_self = dram("v_self", (B, N, D))
    k_ctx = [dram(f"k_parts_ctx{l}", (G, 2, P, B * S)) for l in (0, 1)]
    v_ctx = [dram(f"v_ctx{l}", (B, S, D)) for l in (0, 1)]
    gate_rows = dram("gate_rows", (2, 2, B, D))

    pe, act, dve, pool, sp = (Lane() for _ in range(5))

    def count(name):
        return Count(program.enter_context(nc.semaphore(name)))

    c_const, c_vconst = count("pool_constants"), count("vector_constants")
    c_norm, c_rstd = count("vector_norm_steps"), count("pool_rstd_steps")
    c_turn = count("tensor_transposes")
    c_wide, c_hi, c_lo = count("scalar_float32_values"), count("scalar_hi_parts"), count("vector_lo_parts")
    c_proj, c_res = count("tensor_projections"), count("vector_residuals")
    c_smax, c_negmax = count("tensor_scores_for_max"), count("vector_negated_maxima")
    c_score, c_exp = count("tensor_scores_by_key"), count("scalar_exponentials")
    c_av, c_out = count("tensor_value_sums"), count("vector_normalised_heads")
    c_xb = count("pool_residual_bases")
    c_wlo = count("vector_weight_lo_parts")
    dma_counts = {}

    def dma_count(name):
        if name not in dma_counts:
            dma_counts[name] = count(f"dma_{name}")
        return dma_counts[name]

    def load(name, dst, src):
        return sp.do(lambda e: e.dma_start(dst, src), dma_count(name), 16)

    def raw(ap):
        return ap.bitcast(F32)

    stage_name = ["program"]

    bank = program.enter_context(nc.psum_tensor("banks", [P, 8, 512], F32))

    def sb(ctx, name, shape, dt=F32):
        return ctx.enter_context(nc.sbuf_tensor(f"{stage_name[0]}_{name}", shape, dt))

    ident = sb(program, "identity", [P, P])
    ones = sb(program, "ones", [P, HD])
    minus_half = sb(program, "minus_half", [P, NT])
    MODS = ["L0q_scale", "L0q_shift", "L0kv_scale", "L0kv_shift", "a_shift", "a_scale", "m_shift", "m_scale"]
    mod_col = sb(program, "modulation_columns", [P, len(MODS), KC, B])
    BIAS_COLS = [("L0_bq", D), ("L0_bkv", D), ("L1_b_qkv", 2 * D), ("L1_b_qc", D), ("L1_b_kvc", D), ("L1_b_mlp1", HID)]
    bias_col, at = {}, 0
    n_bias = sum(n for _, n in BIAS_COLS) // P
    bias_cols = sb(program, "bias_columns", [P, n_bias])

    def block():
        with nc.Block() as blk:
            @blk.tensor
            def _(e):
                pe.emit(e)

            @blk.scalar
            def _(e):
                act.emit(e)

            @blk.vector
            def _(e):
                dve.emit(e)

            @blk.gpsimd
            def _(e):
                pool.emit(e)

            @blk.sync
            def _(e):
                for c in dma_counts.values():
                    sp.wait(Tick(c.sem, c.value))
                sp.emit(e)


    def split_weights(ctx, name, w, col0, cols, stage):
        chunks = w.shape[0] // P
        hi, lo = (sb(ctx, f"{name}_{p}", [P, chunks, cols], F32R) for p in ("hi", "lo"))
        ticks = []
        width = min(cols, 1024)
        for c in range(chunks):
            for n in range(0, cols, width):
                i, buf = stage.take(sp)
                t = load(f"stage{i}", buf[:, 0:width], w[c * P:(c + 1) * P, col0 + n:col0 + n + width])
                act.wait(t)
                th = act.do(lambda e, buf=buf, c=c, n=n: e.copy(hi[:, c, n:n + width], buf[:, 0:width]), c_hi)
                dve.wait(t, th)
                tl = dve.do(lambda e, buf=buf, c=c, n=n: e.tensor_tensor(
                    lo[:, c, n:n + width], buf[:, 0:width], raw(hi[:, c, n:n + width]), ALU.subtract), c_wlo)
                stage.free(i, th, tl)
            ticks.append(tl)
        return hi, lo, ticks

    def norm_rows(x, rows, stats, mean_var, rstd, eps, xn, tiles, ready, xn_free):
        dve.wait(*ready)
        for t in tiles:
            r = rows(t)
            s = dve.do(lambda e, t=t, r=r: e.bn_stats(stats[0:r, t, :], x[0:r, t, :]), c_norm)
        dve.wait(s)
        for t in tiles:
            r = rows(t)
            s = dve.do(lambda e, t=t, r=r: e.bn_aggr(mean_var[0:r, t, :], stats[0:r, t, :]), c_norm)
        dve.wait(*xn_free)
        return scale_rows(x, rows, mean_var, rstd, eps, xn, tiles, s)

    def scale_rows(x, rows, mean_var, rstd, eps, xn, tiles, aggregated):
        ticks = []
        pool.wait(aggregated)
        k = 0
        groups = {}
        for t in tiles:
            groups.setdefault(rows(t), []).append(t)
        for r, ts in groups.items():
            t0, t1 = ts[0], ts[-1] + 1
            s = pool.do(lambda e, r=r, t0=t0, t1=t1: e.tensor_scalar(
                rstd[0:r, t0:t1], mean_var[0:r, t0:t1, 1], eps, None, ALU.add), c_rstd)
            pool.wait(s)
            s = pool.do(lambda e, r=r, t0=t0, t1=t1: e.tensor_tensor(
                rstd[0:r, t0:t1], rstd[0:r, t0:t1], minus_half[0:r, 0:t1 - t0], ALU.pow), c_rstd)
        dve.wait(s, aggregated)
        for t in tiles:
            r = rows(t)
            ticks.append(dve.do(lambda e, t=t, r=r: e.tensor_scalar(
                xn[0:r, t, :], x[0:r, t, :], mean_var[0:r, t, 0:1], rstd[0:r, t:t + 1],
                ALU.subtract, ALU.mult), c_norm))
        return ticks

    def parts_of(src, bnk_free, wide, hi, lo, produced, bias=None, scale=1.0):
        act.wait(*produced)
        kw = {} if bias is None and scale == 1.0 else {"bias": 0.0 if bias is None else bias, "scale": scale}
        fn = ACT.Copy if not kw else ACT.Identity
        wi, w = wide.take(act)
        tw = act.do(lambda e: e.activation(w[:, 0:src.shape[1]], src, fn, **kw), c_wide)
        th = act.do(lambda e: e.activation(hi, src, fn, **kw), c_hi)
        dve.wait(th)
        tl = dve.do(lambda e: e.tensor_tensor(lo, w[:, 0:src.shape[1]], raw(hi), ALU.subtract), c_lo)
        wide.free(wi, tl)
        return th, tl

    def turn_batch(xn, xn_ready, xh, xl, xT_free, wide, psum, b, mods):
        done = []
        for c in range(KC):
            i, bk = psum.take(pe)
            pe.wait(*xn_ready)
            for t in range(NT):
                tp = pe.do(lambda e, c=c, t=t, bk=bk: e.transpose(
                    bank[:, bk, t * P:(t + 1) * P], xn[:, t, c * P:(c + 1) * P], ident[:, :]),
                    c_turn if t == NT - 1 else None)
            act.wait(*xT_free)
            dve.wait(*xT_free)
            kw = {}
            if mods:
                sc, sh = (MODS.index(m) for m in mods)
                kw = {"scale": mod_col[:, sc, c, b:b + 1], "bias": mod_col[:, sh, c, b:b + 1]}
            th, tl = parts_of(bank[:, bk, :], None, wide, xh[:, c, :], xl[:, c, :], (tp,), **kw)
            psum.free(i, th)
            done.append((th, tl))
        return done, tp

    def product(out_ap, pairs, signal=c_proj):
        terms = [(l, r) for lh, ll, rh, rl in pairs for l, r in ((lh, rh), (lh, rl), (ll, rh))]
        for k, (l, r) in enumerate(terms):
            last = k == len(terms) - 1
            tick = pe.do(lambda e, l=l, r=r, k=k, last=last: e.matmul(out_ap, l, r, start=k == 0, stop=last),
                         signal if last else None)
        return tick

    with ExitStack() as ctx:
        stage_name[0] = "modulation"
        cond = sb(ctx, "cond_rows", [B, D])
        work = [sb(ctx, f"silu_{n}", [B, D]) for n in ("exp", "one_plus", "recip", "value")]
        cond_T = sb(ctx, "silu_cond_columns", [P, KC, B])
        wbuf = Ring([sb(ctx, f"mod_weights{i}", [P, KC, D]) for i in range(3)])
        bias_rows = sb(ctx, "mod_bias_rows", [B, 10, D])
        proj_bias = [sb(ctx, f"gated_bias_rows{i}", [B, D]) for i in range(2)]
        rows = sb(ctx, "modulation_rows", [B, 10, D])
        gated = sb(ctx, "gate_times_bias", [B, 2, D])
        bias_chunks = sb(ctx, "bias_chunks", [n_bias, P])

        t = pool.do(lambda e: e.memset(ident[:], 0.0), c_const)
        pool.do(lambda e: e.memset(ones[:], 1.0), c_const)
        pool.do(lambda e: e.memset(minus_half[:], -0.5), c_const)
        pool.wait(t)
        const = pool.do(lambda e: e.affine_select(
            out=ident[:], in_=ident[:], compare_op=ALU.not_equal, fill=1.0, base=0,
            pattern=[[-1, P]], channel_multiplier=1), c_const)

        t_cond = load("cond", cond[:], a["cond_1024"])
        sources = [("L0_xcond_Wss_q", "L0_xcond_bss_q", 0), ("L0_xcond_Wss_q", "L0_xcond_bss_q", 1),
                   ("L0_xcond_Wss_kv", "L0_xcond_bss_kv", 0), ("L0_xcond_Wss_kv", "L0_xcond_bss_kv", 1)]
        sources += [("L1_xcond_W_mod", "L1_xcond_b_mod", j) for j in range(6)]
        names = MODS[0:4] + ["a_shift", "a_scale", "a_gate", "m_shift", "m_scale", "m_gate"]
        for j, (_, bname, part) in enumerate(sources):
            t_bias = load("mod_bias", bias_rows[:, j, :],
                          a[bname][part * D:(part + 1) * D].partition_broadcast(B))
        for i, bname in enumerate(("L1_xcond_b_proj", "L1_xcond_b_mlp2")):
            t_bias = load("mod_bias", proj_bias[i][:], a[bname].partition_broadcast(B))
        at = 0
        for bname, n in BIAS_COLS:
            full = bname.replace("_", "_xcond_", 1)
            bias_col[bname] = at
            t_cols = load("bias_chunks", bias_chunks[at:at + n // P, :], a[full][0:n].rearrange("(c p) -> c p", p=P))
            at += n // P

        act.wait(t_cond)
        t = act.do(lambda e: e.activation(work[0][:], cond[:], ACT.Exp, scale=-1.0), c_exp)
        dve.wait(t)
        t = dve.do(lambda e: e.tensor_scalar(work[1][:], work[0][:], 1.0, None, ALU.add), c_norm)
        dve.wait(t)
        t = dve.do(lambda e: e.reciprocal(work[2][:], work[1][:]), c_norm)
        dve.wait(t)
        t = dve.do(lambda e: e.tensor_tensor(work[3][:], cond[:], work[2][:], ALU.mult), c_norm)
        pe.wait(t, const)
        for c in range(KC):
            t = pe.do(lambda e, c=c: e.transpose(bank[:, 7, c * B:(c + 1) * B], work[3][:, c * P:(c + 1) * P],
                                                 ident[0:B, 0:B]), c_turn)
        dve.wait(t)
        t_condT = dve.do(lambda e: e.tensor_copy(cond_T[:], bank[:, 7, 0:KC * B].rearrange("p (c b) -> p c b", b=B)), c_norm)

        pe.wait(t_cols)
        t = pe.do(lambda e: e.transpose(bank[:, 6, 0:n_bias], bias_chunks[:], ident[0:n_bias, 0:n_bias]), c_turn)
        act.wait(t)
        act.do(lambda e: e.copy(bias_cols[:], bank[:, 6, 0:n_bias]), c_wide)

        psum = Ring([0, 1, 2])
        turned = Ring([4, 5])
        for j, (wname, _, part) in enumerate(sources):
            i, w = wbuf.take(sp)
            t_w = load(f"mod_w{i}", w[:], a[wname][:, part * D:(part + 1) * D].rearrange("(c p) n -> p c n", p=P))
            bi, bk = psum.take(pe)
            pe.wait(t_w, t_condT)
            for c in range(KC):
                t = pe.do(lambda e, c=c, w=w, bk=bk: e.matmul(bank[0:B, bk, :], cond_T[:, c, :], w[:, c, :],
                                                             start=c == 0, stop=c == KC - 1), c_proj)
            wbuf.free(i, t)
            dve.wait(t, t_bias)
            one = 1.0 if names[j].endswith("scale") else 0.0
            t = dve.do(lambda e, j=j, bk=bk, one=one: e.scalar_tensor_tensor(
                rows[:, j, :], bank[0:B, bk, :], one, bias_rows[:, j, :], ALU.add, ALU.add), c_norm)
            psum.free(bi, t)
            if names[j].endswith("gate"):
                g = 0 if names[j] == "a_gate" else 1
                t_r = t
                dve.wait(t)
                t = dve.do(lambda e, j=j, g=g: e.tensor_tensor(gated[:, g, :], rows[:, j, :], proj_bias[g][:], ALU.mult), c_norm)
                sp.wait(t_r, t)
                load("gates_out", gate_rows[g, 0], rows[:, j, :])
                load("gates_out", gate_rows[g, 1], gated[:, g, :])
            else:
                m = MODS.index(names[j])
                ti, tb = turned.take(pe)
                pe.wait(t)
                for c in range(KC):
                    t = pe.do(lambda e, c=c, j=j, tb=tb: e.transpose(
                        bank[:, tb, c * B:(c + 1) * B], rows[:, j, c * P:(c + 1) * P], ident[0:B, 0:B]), c_turn)
                dve.wait(t)
                t = dve.do(lambda e, m=m, tb=tb: e.tensor_copy(
                    mod_col[:, m, :, :], bank[:, tb, 0:KC * B].rearrange("p (c b) -> p c b", b=B)), c_norm)
                turned.free(ti, t)
        block()

    with ExitStack() as ctx:
        stage_name[0] = "context"
        CT = B * S
        HALF = CT // 2
        TT = -(-CT // P)
        rows_of = lambda t: min(P, CT - t * P)
        stage = Ring([sb(ctx, f"weight_stage{i}", [P, 1024]) for i in range(2)])
        xc = sb(ctx, "context_rows", [P, TT, D])
        stats, mean_var = sb(ctx, "stats", [P, TT, 6]), sb(ctx, "mean_var", [P, TT, 2])
        rstd = sb(ctx, "rstd", [P, TT])
        xn = sb(ctx, "context_normed", [P, TT, D])
        xT = sb(ctx, "context_turned", [P, KC, CT])
        xh, xl = sb(ctx, "context_hi", [P, KC, CT], F32R), sb(ctx, "context_lo", [P, KC, CT], F32R)
        wide = Ring([sb(ctx, f"wide{i}", [P, 512]) for i in range(2)])
        kst = Ring([sb(ctx, f"key_parts{i}", [P, 2, HALF], F32R) for i in range(2)])
        vst = Ring([sb(ctx, f"value_rows{i}", [S, D]) for i in range(2)])
        bv = [sb(ctx, f"value_bias{l}", [S, D]) for l in (0, 1)]
        flat = a["ctx_1024"].rearrange("b s d -> (b s) d")
        full = CT // P
        load("ctx", xc[:, 0:full, :], flat[0:full * P].rearrange("(t p) d -> p t d", p=P))
        t_x = load("ctx", xc[0:CT - full * P, full, :], flat[full * P:CT])
        wkv = ["L0_xcond_Wkv", "L1_xcond_W_kvc"]
        bkv = ["L0_xcond_bkv", "L1_xcond_b_kvc"]
        for l in (0, 1):
            t_bv = load("value_bias", bv[l][:], a[bkv[l]][D:2 * D].partition_broadcast(S))
        weights = [split_weights(ctx, f"w_kv{l}", a[wkv[l]], 0, 2 * D, stage) for l in (0, 1)]
        psum, proj = Ring([0, 1, 2]), Ring([3, 4, 5])
        parts_free = ()
        xT_free = ()
        xn_free = ()
        for l, eps in ((0, 1e-5), (1, 1e-6)):
            if l == 0:
                ready = norm_rows(xc, rows_of, stats, mean_var, rstd, eps, xn, range(TT), (t_x,), ())
            else:
                dve.wait(*xn_free)
                pool.wait(ready[-1])
                ready = scale_rows(xc, rows_of, mean_var, rstd, eps, xn, range(TT), ready[-1])
            pe.wait(ready[-1])
            for c in range(KC):
                for t0, t1 in ((0, 4), (4, TT)):
                    bi, bk = psum.take(pe)
                    w_ = sum(rows_of(t) for t in range(t0, t1))
                    for t in range(t0, t1):
                        r = rows_of(t)
                        tp = pe.do(lambda e, c=c, t=t, r=r, bk=bk, t0=t0: e.transpose(
                            bank[:, bk, (t - t0) * P:(t - t0) * P + r], xn[0:r, t, c * P:(c + 1) * P],
                            ident[0:r, 0:r]), c_turn)
                    act.wait(tp, *xT_free)
                    tw = act.do(lambda e, c=c, t0=t0, w_=w_, bk=bk: e.activation(
                        xT[:, c, t0 * P:t0 * P + w_], bank[:, bk, 0:w_], ACT.Copy), c_wide)
                    psum.free(bi, tw)
            xn_free = (tp,)
            act.wait(tw)
            if l == 0:
                for c in range(KC):
                    for b in range(B):
                        tw = act.do(lambda e, c=c, b=b: e.activation(
                            xT[:, c, b * S:(b + 1) * S], xT[:, c, b * S:(b + 1) * S], ACT.Identity,
                            bias=mod_col[:, 3, c, b:b + 1], scale=mod_col[:, 2, c, b:b + 1]), c_wide)
                act.wait(tw)
            for c in range(KC):
                act.wait(*parts_free)
                th = act.do(lambda e, c=c: e.copy(xh[:, c, :], xT[:, c, :]), c_hi)
                dve.wait(th, *parts_free)
                tl = dve.do(lambda e, c=c: e.tensor_tensor(xl[:, c, :], xT[:, c, :], raw(xh[:, c, :]), ALU.subtract), c_lo)
            xT_free = (tl,)
            wh, wl, tw_ = weights[l]
            pe.wait(th, tl, *tw_)
            bcol = bias_col["L0_bkv" if l == 0 else "L1_b_kvc"]
            for g in range(G):
                for h in range(2):
                    bi, bk = proj.take(pe)
                    cols = slice(h * HALF, (h + 1) * HALF)
                    f = slice(g * P, (g + 1) * P)
                    tp = product(bank[:, bk, 0:HALF], [(wh[:, c, f], wl[:, c, f], xh[:, c, cols], xl[:, c, cols])
                                                      for c in range(KC)])
                    ki, kt = kst.take(act, dve)
                    th, tl = parts_of(bank[:, bk, 0:HALF], None, wide, kt[:, 0, :], kt[:, 1, :], (tp,),
                                      bias=bias_cols[:, bcol + g:bcol + g + 1])
                    proj.free(bi, th)
                    sp.wait(th, tl)
                    t = load(f"key_store{ki}", k_ctx[l][g, :, :, cols].rearrange("s p t -> p s t"), raw(kt[:]))
                    kst.free(ki, t)
            for b in range(B):
                bi, bk = proj.take(pe)
                r = slice(b * S, (b + 1) * S)
                tp = product(bank[0:S, bk, :], [(xh[:, c, r], xl[:, c, r], wh[:, c, D:2 * D], wl[:, c, D:2 * D])
                                               for c in range(KC)])
                vi, vt = vst.take(dve)
                dve.wait(tp, t_bv)
                t = dve.do(lambda e, bk=bk, l=l, vt=vt: e.tensor_tensor(vt[:], bank[0:S, bk, :], bv[l][:], ALU.add), c_res)
                proj.free(bi, t)
                sp.wait(t)
                vst.free(vi, load(f"value_store{vi}", v_ctx[l][b], vt[:]))
            parts_free = (tp,)
        block()

    def attention_stage(name, x_in, x_out, wq, bq, wp, bp, mods, eps, layer):
        own_q = layer is not None
        keys = S if own_q else P
        KT = 1 if own_q else NT
        with ExitStack() as ctx:
            stage_name[0] = name
            x_ring = Ring([sb(ctx, f"x_rows{i}", [P, NT, D]) for i in range(2)])
            q_ring = Ring([sb(ctx, f"query_stack{i}", [ST_MAX, GH, N], F32R) for i in range(3)])
            if own_q:
                k_ring = Ring([sb(ctx, f"key_stack{i}", [ST_MAX, NH, SP_], F32R) for i in range(2)])
            else:
                k_ring = Ring([sb(ctx, f"key_stack{i}", [ST_MAX, GH, N], F32R) for i in range(3)])
            v_ring = Ring([sb(ctx, f"values{i}", [keys, KT, D]) for i in range(2)])
            p_ring = Ring([sb(ctx, f"exponentials{i}", [keys, GH, N]) for i in range(2 if own_q else 4)])
            o_ring = Ring([(sb(ctx, f"heads_hi{i}", [P, G, N], F32R), sb(ctx, f"heads_lo{i}", [P, G, N], F32R))
                           for i in range(2)])
            recip = sb(ctx, "reciprocal_sums", [P, N])
            o_wide = Ring([sb(ctx, f"heads_float32_{i}", [P, N]) for i in range(2)])
            negmax = Ring([sb(ctx, f"negated_max{i}", [P, GH * NT]) for i in range(2)])
            max_rows = Ring([sb(ctx, f"max_row_parts{i}", [GH * NT, 2, P], F32R) for i in range(2)])
            for i, k in enumerate(k_ring.slots):
                if own_q:
                    dve.do(lambda e, k=k: e.memset(raw(k[0:ST]), 0.0), c_vconst)
                t_ones = dve.do(lambda e, k=k: e.memset(raw(k[ST:ST_MAX]), 1.0), c_vconst)
                k_ring.free(i, t_ones)
            stage = Ring([sb(ctx, f"weight_stage{i}", [P, 512]) for i in range(2)])
            if own_q:
                wide = Ring([sb(ctx, f"wide{i}", [P, N]) for i in range(2)])
                stats, mean_var = sb(ctx, "stats", [P, NT, 6]), sb(ctx, "mean_var", [P, NT, 2])
                rstd = sb(ctx, "rstd", [P, NT])
                xn = sb(ctx, "x_normed", [P, NT, D])
                xh, xl = sb(ctx, "x_hi", [P, KC, N], F32R), sb(ctx, "x_lo", [P, KC, N], F32R)
                q_out = Ring([sb(ctx, f"query_parts{i}", [P, 2, N], F32R) for i in range(2)])
                wqh, wql, t_wq = split_weights(ctx, "w_q", wq, 0, D, stage)
                bias_tile = sb(ctx, "projection_bias", [P, D])
                t_bias = load("projection_bias", bias_tile[:], bp.partition_broadcast(P))
            else:
                gate = Ring([sb(ctx, f"gate_and_bias{i}", [P, 2, D]) for i in range(2)])
                gated_rows = Ring([sb(ctx, f"gated_rows{i}", [P, D]) for i in range(2)])
            wph, wpl, t_wp = split_weights(ctx, "w_proj", wp, 0, D, stage)

            proj, smax, score, heads, sums = Ring([0, 1]), Ring([2, 3]), Ring([4, 5]), Ring([6]), Ring([7])
            free = {"xn": (), "parts": ()}
            batch, group = {}, {}

            def load_batch(b):
                st = batch[b] = {}
                st["xi"], st["x"] = x_ring.take(sp)
                st["t_x"] = load(f"x{st['xi']}", st["x"][:], x_in[b].rearrange("(t p) d -> p t d", p=P))
                st["vi"], st["v"] = v_ring.take(sp)
                if own_q:
                    st["t_v"] = load(f"v{st['vi']}", st["v"][:, 0, :], v_ctx[layer][b])
                    st["ki"], st["k"] = k_ring.take(sp)
                    src = k_ctx[layer][:, :, :, b * S:(b + 1) * S].rearrange("g s (h p) t -> s p g h t", p=HD)
                    for r, s in ((0, 0), (1, 0), (2, 1)):
                        for g in range(G):
                            st["t_k"] = load(f"k{st['ki']}", raw(st["k"][r * HD:(r + 1) * HD, g * GH:(g + 1) * GH, 0:S]), src[s, :, g])
                else:
                    st["t_v"] = load(f"v{st['vi']}", st["v"][:], v_self[b].rearrange("(t p) d -> p t d", p=P))
                    st["gi"], st["gate"] = gate.take(sp)
                    for w in range(2):
                        st["t_gate"] = load(f"gate{st['gi']}", st["gate"][:, w, :],
                                            gate_rows[0, w, b].partition_broadcast(P))

            def norm_batch(b):
                st = batch[b]
                ready = norm_rows(st["x"], lambda t: P, stats, mean_var, rstd, eps, xn, range(NT), (st["t_x"],), free["xn"])
                st["parts"], t = turn_batch(xn, ready, xh, xl, free["parts"], wide, proj, b, mods)
                free["xn"] = (t,)
                st["normed"] = ready

            def base_batch(b):
                st = batch[b]
                if own_q:
                    pool.wait(*st["normed"], t_bias)
                    rhs = lambda t: bias_tile[:]
                else:
                    pool.wait(st["t_x"], st["t_gate"])
                    rhs = lambda t: st["gate"][:, 1, :]
                for t in range(NT):
                    st["t_base"] = pool.do(lambda e, t=t: e.tensor_tensor(
                        st["x"][:, t, :], st["x"][:, t, :], rhs(t), ALU.add), c_xb)

            def query(b, g):
                st = batch[b]
                pi, bk = proj.take(pe)
                pe.wait(*t_wq, *(t for pair in st["parts"] for t in pair))
                f = slice(g * P, (g + 1) * P)
                tp = product(bank[:, bk, :], [(wqh[:, c, f], wql[:, c, f], xh[:, c, :], xl[:, c, :]) for c in range(KC)])
                if g == G - 1:
                    free["parts"] = (tp,)
                qi, qt = q_out.take(act, dve)
                th, tl = parts_of(bank[:, bk, :], None, wide, qt[:, 0, :], qt[:, 1, :], (tp,),
                                  bias=bias_cols[:, bias_col[bq] + g:bias_col[bq] + g + 1])
                proj.free(pi, th)
                sp.wait(th, tl)
                t = load(f"q_store{qi}", q_parts[name][b, g].rearrange("s p t -> p s t"), raw(qt[:]))
                q_out.free(qi, t)
                group[b, g] = {"stored": t}

            def fetch(b, g):
                gr = group.setdefault((b, g), {"stored": None})
                sp.wait(gr["stored"])
                gr["qi"], gr["q"] = q_ring.take(sp)
                src = q_parts[name][b, g].rearrange("s (h p) t -> s p h t", p=HD)
                for r, s in enumerate((0, 1, 0)):
                    gr["t_q"] = load(f"q{gr['qi']}", raw(gr["q"][r * HD:(r + 1) * HD]), src[s])
                if own_q:
                    gr["k"] = batch[b]["k"][:, g * GH:(g + 1) * GH, :]
                    gr["t_k"] = batch[b]["t_k"]
                else:
                    gr["ki"], gr["k"] = k_ring.take(sp)
                    src = k_self[b, g].rearrange("s (h p) t -> s p h t", p=HD)
                    for r, s in enumerate((0, 0, 1)):
                        gr["t_k"] = load(f"k{gr['ki']}", raw(gr["k"][r * HD:(r + 1) * HD]), src[s])

            def maxima(b, g):
                gr = group[b, g]
                ni, nm = negmax.take(dve)
                pe.wait(gr["t_q"], gr["t_k"])
                for qt in range(NT):
                    rows = slice(qt * P, (qt + 1) * P)
                    if own_q:
                        si, bk = smax.take(pe)
                        for h in range(GH):
                            tp = pe.do(lambda e, h=h, bk=bk, rows=rows: e.matmul(
                                bank[:, bk, h * SP_:(h + 1) * SP_], gr["q"][0:ST, h, rows], gr["k"][0:ST, h, :],
                                start=True, stop=True), c_smax)
                        dve.wait(tp)
                        tn = dve.do(lambda e, bk=bk, qt=qt: e.tensor_reduce(
                            nm[:, qt:GH * NT:NT], bank[:, bk, 0:GH * SP_].rearrange("p (h k) -> p h k", k=SP_)[:, :, 0:S],
                            AX_X, ALU.max, negate=True), c_negmax)
                        smax.free(si, tn)
                        yield
                    else:
                        for h in range(GH):
                            si, bk = smax.take(pe)
                            tp = pe.do(lambda e, h=h, bk=bk, rows=rows: e.matmul(
                                bank[:, bk, :], gr["q"][0:ST, h, rows], gr["k"][0:ST, h, :],
                                start=True, stop=True), c_smax)
                            dve.wait(tp)
                            tn = dve.do(lambda e, bk=bk, qt=qt, h=h: e.tensor_reduce(
                                nm[:, h * NT + qt:h * NT + qt + 1], bank[:, bk, :], AX_X, ALU.max, negate=True), c_negmax)
                            smax.free(si, tn)
                            yield
                si, bk = smax.take(pe)
                pe.wait(tn)
                tp = pe.do(lambda e: e.transpose(bank[0:GH * NT, bk, 0:P], nm[:], ident[:]), c_turn)
                negmax.free(ni, tp)
                mi, mr = max_rows.take(act, dve)
                act.wait(tp)
                th = act.do(lambda e: e.activation(mr[:, 0, :], bank[0:GH * NT, bk, 0:P], ACT.Copy), c_hi)
                dve.wait(th)
                tl = dve.do(lambda e: e.tensor_tensor(mr[:, 1, :], bank[0:GH * NT, bk, 0:P], raw(mr[:, 0, :]), ALU.subtract), c_lo)
                smax.free(si, tl)
                sp.wait(th, tl, tp)
                for w in range(2):
                    gr["t_max"] = load(f"max{gr['qi']}", raw(gr["q"][ST + w:ST + w + 1].rearrange("a h (t q) -> a (h t) q", q=P)),
                                       raw(mr[:, w, :]))
                max_rows.free(mi, gr["t_max"])

            def attend(b, g):
                gr, st = group[b, g], batch[b]
                pe.wait(gr["t_max"])
                _, ob = heads.take(pe)
                _, sb_ = sums.take(pe)
                for kt in range(KT):
                    pi, pt = p_ring.take(act)
                    cols = slice(kt * P, kt * P + keys)
                    for h in range(GH):
                        si, bk = score.take(pe)
                        tp = pe.do(lambda e, h=h, bk=bk, cols=cols: e.matmul(
                            bank[0:keys, bk, :], gr["k"][0:ST_MAX, h, cols], gr["q"][0:ST_MAX, h, :],
                            start=True, stop=True), c_score)
                        act.wait(tp)
                        te = act.do(lambda e, h=h, bk=bk, pt=pt: e.activation(
                            pt[:, h, :], bank[0:keys, bk, :], ACT.Exp, scale=SCALE), c_exp)
                        score.free(si, te)
                        yield
                    if kt == KT - 1:
                        q_ring.free(gr["qi"], tp)
                        if not own_q:
                            k_ring.free(gr["ki"], tp)
                        elif g == G - 1:
                            k_ring.free(st["ki"], tp)
                    if kt > 0:
                        values(b, g, kt - 1, prev, ob, sb_)
                        yield
                    prev = (pi, pt, te)
                gr["last"] = (prev, ob, sb_)

            def values(b, g, kt, prev, ob, sb_):
                pi, pt, te = prev
                st = batch[b]
                pe.wait(te, st["t_v"])
                for lhs, bk in ((None, ob), (ones, sb_)):
                    for h in range(GH):
                        f = (g * GH + h) * HD
                        w = st["v"][:, kt, f:f + HD] if lhs is None else ones[0:keys, :]
                        tp = pe.do(lambda e, h=h, bk=bk, w=w: e.matmul(
                            bank[h * HD:(h + 1) * HD, bk, :], w, pt[:, h, :],
                            start=kt == 0, stop=kt == KT - 1), c_av)
                p_ring.free(pi, tp)
                return tp

            def finish(b, g):
                gr, st = group[b, g], batch[b]
                prev, ob, sb_ = gr["last"]
                tp = values(b, g, KT - 1, prev, ob, sb_)
                if g == 0:
                    st["oi"], st["o"] = o_ring.take(act, dve)
                if g == G - 1:
                    v_ring.free(st["vi"], tp)
                dve.wait(tp)
                tr = dve.do(lambda e: e.reciprocal(recip[:], bank[:, sb_, :]), c_out)
                dve.wait(tr)
                wi, w = o_wide.take(dve)
                to = dve.do(lambda e: e.tensor_tensor(w[:], bank[:, ob, :], recip[:], ALU.mult), c_out)
                heads.free(0, to)
                sums.free(0, to)
                oh, ol = st["o"]
                act.wait(to)
                th = act.do(lambda e: e.copy(oh[:, g, :], w[:]), c_hi)
                gr["split"] = (th, w, wi)

            def finish_lo(b, g):
                gr, st = group[b, g], batch[b]
                th, w, wi = gr["split"]
                oh, ol = st["o"]
                dve.wait(th)
                tl = dve.do(lambda e: e.tensor_tensor(ol[:, g, :], w[:], raw(oh[:, g, :]), ALU.subtract), c_lo)
                o_wide.free(wi, tl)
                st["t_o"] = (th, tl)

            def project(b):
                st = batch[b]
                oh, ol = st["o"]
                pe.wait(*st["t_o"], *t_wp)
                for t in range(NT):
                    pi, bk = proj.take(pe)
                    r = slice(t * P, (t + 1) * P)
                    tp = product(bank[:, bk, :], [(oh[:, c, r], ol[:, c, r], wph[:, c, :], wpl[:, c, :]) for c in range(KC)])
                    dve.wait(tp, st["t_base"])
                    if own_q:
                        tres = dve.do(lambda e, t=t, bk=bk: e.tensor_tensor(
                            st["x"][:, t, :], bank[:, bk, :], st["x"][:, t, :], ALU.add), c_res)
                        proj.free(pi, tres)
                    else:
                        dve.wait(st["t_gate"])
                        wi, w = gated_rows.take(dve)
                        tg = dve.do(lambda e, bk=bk, w=w: e.tensor_tensor(w[:], bank[:, bk, :], st["gate"][:, 0, :], ALU.mult), c_res)
                        proj.free(pi, tg)
                        dve.wait(tg)
                        tres = dve.do(lambda e, t=t, w=w: e.tensor_tensor(
                            st["x"][:, t, :], w[:], st["x"][:, t, :], ALU.add), c_res)
                        gated_rows.free(wi, tres)
                o_ring.free(st["oi"], tp)
                if not own_q:
                    gate.free(st["gi"], tres, st["t_base"])
                sp.wait(tres)
                x_ring.free(st["xi"], load(f"x_out{st['xi']}", x_out[b].rearrange("(t p) d -> p t d", p=P), st["x"][:]))

            seq = [(b, g) for b in range(B) for g in range(G)]
            AHEAD = 2
            load_batch(0)
            if own_q:
                norm_batch(0)
            base_batch(0)
            for n in range(AHEAD):
                if own_q:
                    query(*seq[n])
            fetch(*seq[0])
            for _ in maxima(*seq[0]):
                pass
            fetch(*seq[1])
            for n, (b, g) in enumerate(seq):
                if g == 1 and b + 1 < B:
                    load_batch(b + 1)
                    if not own_q:
                        base_batch(b + 1)
                if own_q and n + AHEAD < len(seq):
                    if seq[n + AHEAD][1] == 0:
                        norm_batch(seq[n + AHEAD][0])
                        base_batch(seq[n + AHEAD][0])
                    query(*seq[n + AHEAD])
                if n + 2 < len(seq):
                    fetch(*seq[n + 2])
                steps = [attend(b, g)]
                if n + 1 < len(seq):
                    steps.append(maxima(*seq[n + 1]))
                while steps:
                    for s in list(steps):
                        try:
                            next(s)
                        except StopIteration:
                            steps.remove(s)
                finish(b, g)
                if g == 0 and b > 0:
                    project(b - 1)
                finish_lo(b, g)
            project(B - 1)
            block()

    attention_stage("L0", a["x"], x1, a["L0_xcond_Wq"], "L0_bq", a["L0_xcond_Wp"], a["L0_xcond_bp"],
                    ("L0q_scale", "L0q_shift"), 1e-5, 0)

    with ExitStack() as ctx:
        stage_name[0] = "qkv"
        x_ring = Ring([sb(ctx, f"x_rows{i}", [P, NT, D]) for i in range(2)])
        stage = Ring([sb(ctx, f"weight_stage{i}", [P, 1024]) for i in range(2)])
        wide = Ring([sb(ctx, f"wide{i}", [P, N]) for i in range(2)])
        stats, mean_var = sb(ctx, "stats", [P, NT, 6]), sb(ctx, "mean_var", [P, NT, 2])
        rstd = sb(ctx, "rstd", [P, NT])
        xn = sb(ctx, "x_normed", [P, NT, D])
        parts = [(sb(ctx, f"x_hi{i}", [P, KC, N], F32R), sb(ctx, f"x_lo{i}", [P, KC, N], F32R)) for i in range(2)]
        parts_free = [(), ()]
        o_parts = Ring([sb(ctx, f"qk_parts{i}", [P, 2, N], F32R) for i in range(3)])
        v_rows = Ring([sb(ctx, f"value_rows{i}", [P, D]) for i in range(2)])
        bias_tile = sb(ctx, "value_bias_tile", [P, D])
        t_bias = load("value_bias", bias_tile[:], a["L1_xcond_b_qkv"][2 * D:3 * D].partition_broadcast(P))
        wk_h, wk_l, t_wk = split_weights(ctx, "w_qk", a["L1_xcond_W_qkv"], 0, 2 * D, stage)
        wv_h, wv_l, t_wv = split_weights(ctx, "w_v", a["L1_xcond_W_qkv"], 2 * D, D, stage)
        turn, proj = Ring([0, 1, 2]), Ring([3, 4, 5, 6])
        xn_free = ()

        def normed(b):
            nonlocal xn_free
            i, x = x_ring.take(sp)
            t = load(f"x{i}", x[:], x1[b].rearrange("(t p) d -> p t d", p=P))
            ready = norm_rows(x, lambda t: P, stats, mean_var, rstd, 1e-6, xn, range(NT), (t,), xn_free)
            x_ring.free(i, ready[-1])
            done, tp = turn_batch(xn, ready, *parts[b % 2], parts_free[b % 2], wide, turn, b, ("a_scale", "a_shift"))
            xn_free = (tp,)
            return done

        done = normed(0)
        for b in range(B):
            xh, xl = parts[b % 2]
            pe.wait(*(t for pair in done for t in pair), *t_wk)
            for m in range(2 * G):
                pi, bk = proj.take(pe)
                f = slice(m * P, (m + 1) * P)
                tp = product(bank[:, bk, :], [(wk_h[:, c, f], wk_l[:, c, f], xh[:, c, :], xl[:, c, :]) for c in range(KC)])
                oi, ot = o_parts.take(act, dve)
                col = bias_col["L1_b_qkv"] + m
                th, tl = parts_of(bank[:, bk, :], None, wide, ot[:, 0, :], ot[:, 1, :], (tp,), bias=bias_cols[:, col:col + 1])
                proj.free(pi, th)
                sp.wait(th, tl)
                dst = q_parts["self"] if m < G else k_self
                o_parts.free(oi, load(f"qk_store{oi}", dst[b, m % G].rearrange("s p t -> p s t"), raw(ot[:])))
                if m == 2 and b + 1 < B:
                    done = normed(b + 1)
            pe.wait(*t_wv)
            for t in range(NT):
                pi, bk = proj.take(pe)
                r = slice(t * P, (t + 1) * P)
                tp = product(bank[:, bk, :], [(xh[:, c, r], xl[:, c, r], wv_h[:, c, :], wv_l[:, c, :]) for c in range(KC)])
                vi, vt = v_rows.take(dve)
                dve.wait(tp, t_bias)
                tv = dve.do(lambda e, bk=bk, vt=vt: e.tensor_tensor(vt[:], bank[:, bk, :], bias_tile[:], ALU.add), c_res)
                proj.free(pi, tv)
                sp.wait(tv)
                v_rows.free(vi, load(f"value_store{vi}", v_self[b, r, :], vt[:]))
            parts_free[b % 2] = (tp,)
        block()

    attention_stage("self", x1, x2, None, None, a["L1_xcond_W_proj"], None, None, None, None)
    attention_stage("cross", x2, x3, a["L1_xcond_W_qc"], "L1_b_qc", a["L1_xcond_W_cproj"], a["L1_xcond_b_cproj"],
                    None, 1e-6, 1)

    with ExitStack() as ctx:
        stage_name[0] = "mlp"
        JC = HID // P
        x_ring = Ring([sb(ctx, f"x_rows{i}", [P, NT, D]) for i in range(1)])
        stage = Ring([sb(ctx, f"weight_stage{i}", [P, 1024]) for i in range(1)])
        wide = Ring([sb(ctx, f"wide{i}", [P, N]) for i in range(2)])
        stats, mean_var = sb(ctx, "stats", [P, NT, 6]), sb(ctx, "mean_var", [P, NT, 2])
        rstd = sb(ctx, "rstd", [P, NT])
        xn = sb(ctx, "x_normed", [P, NT, D])
        xh, xl = sb(ctx, "x_hi", [P, KC, N], F32R), sb(ctx, "x_lo", [P, KC, N], F32R)
        h_parts = Ring([sb(ctx, f"hidden_parts{i}", [P, 2, N], F32R) for i in range(3)])
        gate = Ring([sb(ctx, f"gate_and_bias{i}", [P, 2, D]) for i in range(1)])
        prod = Ring([sb(ctx, f"gated_rows{i}", [P, D]) for i in range(1)])
        w1h, w1l, t_w1 = split_weights(ctx, "w_mlp1", a["L1_xcond_W_mlp1"], 0, HID, stage)
        w2h, w2l, t_w2 = split_weights(ctx, "w_mlp2", a["L1_xcond_W_mlp2"], 0, D, stage)
        acc = [4, 5, 6, 7]
        up, turn = Ring([0, 1]), Ring([2, 3])
        acc_free = [()] * NT
        parts_free, xn_free = (), ()
        for b in range(B):
            xi, x = x_ring.take(sp)
            t_x = load(f"x{xi}", x[:], x3[b].rearrange("(t p) d -> p t d", p=P))
            gi, gt = gate.take(sp)
            for w in range(2):
                t_g = load(f"gate{gi}", gt[:, w, :], gate_rows[1, w, b].partition_broadcast(P))
            ready = norm_rows(x, lambda t: P, stats, mean_var, rstd, 1e-6, xn, range(NT), (t_x,), xn_free)
            done, tp = turn_batch(xn, ready, xh, xl, parts_free, wide, turn, b, ("m_scale", "m_shift"))
            xn_free = (tp,)
            pool.wait(*ready, t_g)
            for t in range(NT):
                t_base = pool.do(lambda e, t=t, x=x, gt=gt: e.tensor_tensor(x[:, t, :], x[:, t, :], gt[:, 1, :], ALU.add), c_xb)
            pe.wait(*(t for pair in done for t in pair), *t_w1)
            pending = []

            def down(j, hi_, ht, ticks):
                pe.wait(*ticks, t_w2[j])
                for t in range(NT):
                    if j == 0:
                        pe.wait(*acc_free[t])
                    r = slice(t * P, (t + 1) * P)
                    terms = [(ht[:, 0, r], w2h[:, j, :]), (ht[:, 0, r], w2l[:, j, :]), (ht[:, 1, r], w2h[:, j, :])]
                    for k, (l, w) in enumerate(terms):
                        tick = pe.do(lambda e, l=l, w=w, k=k, t=t: e.matmul(
                            bank[:, acc[t], :], l, w, start=j == 0 and k == 0, stop=j == JC - 1 and k == 2), c_proj)
                h_parts.free(hi_, tick)
                return tick

            for j in range(JC):
                ui, bk = up.take(pe)
                f = slice(j * P, (j + 1) * P)
                tp = product(bank[:, bk, :], [(w1h[:, c, f], w1l[:, c, f], xh[:, c, :], xl[:, c, :]) for c in range(KC)])
                wi, w = wide.take(act)
                hi_, ht = h_parts.take(act, dve)
                act.wait(tp)
                col = bias_col["L1_b_mlp1"] + j
                tw = act.do(lambda e, w=w, bk=bk, col=col: e.activation(w[:], bank[:, bk, :], ACT.Gelu_apprx_tanh,
                                                               bias=bias_cols[:, col:col + 1]), c_wide)
                up.free(ui, tw)
                act.wait(tw)
                th = act.do(lambda e, w=w, ht=ht: e.copy(ht[:, 0, :], w[:]), c_hi)
                dve.wait(th)
                tl = dve.do(lambda e, w=w, ht=ht: e.tensor_tensor(ht[:, 1, :], w[:], raw(ht[:, 0, :]), ALU.subtract), c_lo)
                wide.free(wi, tl)
                pending.append((j, hi_, ht, (th, tl)))
                if len(pending) > 1:
                    down(*pending.pop(0))
            parts_free = (tp,)
            tick = down(*pending.pop(0))
            for t in range(NT):
                pi, pr = prod.take(dve)
                dve.wait(tick, t_g, t_base)
                tg = dve.do(lambda e, t=t, pr=pr, gt=gt: e.tensor_tensor(pr[:], bank[:, acc[t], :], gt[:, 0, :], ALU.mult), c_res)
                acc_free[t] = (tg,)
                dve.wait(tg)
                tres = dve.do(lambda e, t=t, pr=pr, x=x: e.tensor_tensor(x[:, t, :], pr[:], x[:, t, :], ALU.add), c_res)
                prod.free(pi, tres)
            gate.free(gi, tres, t_base)
            sp.wait(tres)
            x_ring.free(xi, load(f"x_out{xi}", out[b].rearrange("(t p) d -> p t d", p=P), x[:]))
        block()


_INS = ["x", "ctx_1024", "cond_1024"] + ["L0_xcond_" + n for n in (
    "Wq", "bq", "Wkv", "bkv", "Wp", "bp", "Wss_q", "bss_q", "Wss_kv", "bss_kv")] + ["L1_xcond_" + n for n in (
    "W_mod", "b_mod", "W_qkv", "b_qkv", "W_proj", "b_proj", "W_qc", "b_qc", "W_kvc", "b_kvc", "W_cproj", "b_cproj",
    "W_mlp1", "b_mlp1", "W_mlp2", "b_mlp2")]


def kernel(**inputs):
    import numpy as _np
    import concourse.bacc as _bacc
    from concourse import mybir as _mybir
    from concourse.bass_utils import run_bass_kernel_spmd as _run

    nc = _bacc.Bacc("TRN2", target_bir_lowering=False, num_devices=1)
    arrays, args = {}, {}
    for name in _INS:
        v = _np.ascontiguousarray(inputs[name])
        arrays[f"in_{name}"] = v
        args[name] = nc.dram_tensor(f"in_{name}", v.shape, _mybir.dt.from_np(v.dtype), kind="ExternalInput").ap()
    out = nc.dram_tensor("out", (B, N, D), F32, kind="ExternalOutput").ap()
    build(nc, args, out)
    r = _run(nc, [arrays], core_ids=[0])
    return r.results[0]["out"]
```

```python
from contextlib import ExitStack

import numpy as np

import concourse.bass as bass
from concourse import mybir

F32 = mybir.dt.float32
F32R = mybir.dt.float32r
ALU = mybir.AluOpType
ACT = mybir.ActivationFunctionType
AX_X = mybir.AxisListType.X

P = 128
B, N, D = 8, 512, 512
S = 77
NH, HD = 16, 32
GH = P // HD
G = NH // GH
KC = D // P
NT = N // P
HID = 4 * D
SCALE = float(HD) ** -0.5
ST = 3 * HD
ST_MAX = ST + 2
SP_ = S + 1


class Tick:

    def __init__(self, sem, value):
        self.sem, self.value = sem, value


class Count:

    def __init__(self, sem):
        self.sem, self.value = sem, 0

    def next(self, by):
        self.value += by
        return Tick(self.sem, self.value)


class Lane:

    def __init__(self):
        self.queue, self.waited = [], {}

    def wait(self, *ticks):
        for t in ticks:
            if t is not None and self.waited.get(id(t.sem), 0) < t.value:
                self.waited[id(t.sem)] = t.value
                self.queue.append(lambda e, t=t: e.wait_ge(t.sem, t.value))

    def do(self, make, signal=None, by=1):
        tick = signal.next(by) if signal is not None else None
        if tick is None:
            self.queue.append(make)
        else:
            self.queue.append(lambda e: make(e).then_inc(tick.sem, by))
        return tick

    def emit(self, engine):
        for make in self.queue:
            make(engine)
        self.queue = []


class Ring:

    def __init__(self, slots):
        self.slots, self.freed = list(slots), [()] * len(slots)
        self.idle = list(range(len(slots)))

    def take(self, *writers):
        i = self.idle.pop(0)
        for lane in writers:
            lane.wait(*self.freed[i])
        return i, self.slots[i]

    def free(self, i, *ticks):
        self.freed[i] = ticks
        if i not in self.idle:
            self.idle.append(i)


def build(nc, a, out):
    with ExitStack() as program:
        _build(nc, a, out, program)


def _build(nc, a, out, program):
    def dram(name, shape):
        return nc.dram_tensor(name, shape, F32, kind="Internal").ap()

    x1, x2, x3 = (dram(f"x{i}", (B, N, D)) for i in (1, 2, 3))
    q_parts = {s: dram(f"q_parts_{s}", (B, G, 2, HD, GH, N)) for s in ("L0", "self", "cross")}
    k_self = dram("k_parts_self", (B, G, 2, HD, GH, N))
    v_self = dram("v_self", (B, N, D))
    k_ctx = [dram(f"k_parts_ctx{l}", (2, D, B * S)) for l in (0, 1)]
    v_ctx = [dram(f"v_ctx{l}", (B, S, D)) for l in (0, 1)]
    gate_rows = dram("gate_rows", (2, 2, B, D))

    pe, act, dve, pool, sp = (Lane() for _ in range(5))

    def count(name):
        return Count(program.enter_context(nc.semaphore(name)))

    c_const, c_vconst = count("pool_constants"), count("vector_constants")
    c_norm, c_rstd = count("vector_norm_steps"), count("pool_rstd_steps")
    c_turn = count("tensor_transposes")
    c_wide, c_hi, c_lo = count("scalar_float32_values"), count("scalar_hi_parts"), count("vector_lo_parts")
    c_proj, c_res = count("tensor_projections"), count("vector_residuals")
    c_smax, c_negmax = count("tensor_scores_for_max"), count("vector_negated_maxima")
    c_score, c_exp = count("tensor_scores_by_key"), count("scalar_exponentials")
    c_av, c_out = count("tensor_value_sums"), count("vector_normalised_heads")
    c_xb = count("pool_residual_bases")
    c_wlo = count("vector_weight_lo_parts")
    dma_counts = {}

    def dma_count(name):
        if name not in dma_counts:
            dma_counts[name] = count(f"dma_{name}")
        return dma_counts[name]

    def load(name, dst, src):
        return sp.do(lambda e: e.dma_start(dst, src), dma_count(name), 16)

    def raw(ap):
        return ap.bitcast(F32)

    stage_name = ["program"]

    def store_parts(name, dst, tile):
        for s in range(2):
            t = load(name, dst[s].rearrange("p h t -> h p t"), raw(tile[:, s, :]))
        return t

    bank = program.enter_context(nc.psum_tensor("banks", [P, 8, 512], F32))

    def sb(ctx, name, shape, dt=F32):
        return ctx.enter_context(nc.sbuf_tensor(f"{stage_name[0]}_{name}", shape, dt))

    ident = sb(program, "identity", [P, P])
    ones = sb(program, "ones", [P, HD])
    minus_half = sb(program, "minus_half", [P, NT])
    MODS = ["L0q_scale", "L0q_shift", "L0kv_scale", "L0kv_shift", "a_shift", "a_scale", "m_shift", "m_scale"]
    mod_col = sb(program, "modulation_columns", [P, len(MODS), KC, B])
    BIAS_COLS = [("L0_bq", D), ("L0_bkv", D), ("L1_b_qkv", 2 * D), ("L1_b_qc", D), ("L1_b_kvc", D), ("L1_b_mlp1", HID)]
    bias_col, at = {}, 0
    n_bias = sum(n for _, n in BIAS_COLS) // P
    bias_cols = sb(program, "bias_columns", [P, n_bias])

    def block():
        with nc.Block() as blk:
            @blk.tensor
            def _(e):
                pe.emit(e)

            @blk.scalar
            def _(e):
                act.emit(e)

            @blk.vector
            def _(e):
                dve.emit(e)

            @blk.gpsimd
            def _(e):
                pool.emit(e)

            @blk.sync
            def _(e):
                for c in dma_counts.values():
                    sp.wait(Tick(c.sem, c.value))
                sp.emit(e)


    class Weights:

        def __init__(self, ctx, name, w, col0, cols, stage):
            self.w, self.col0, self.cols, self.stage, self.chunks = w, col0, cols, stage, w.shape[0] // P
            self.hi, self.lo = (sb(ctx, f"{name}_{p}", [P, self.chunks, cols], F32R) for p in ("hi", "lo"))
            self.ready = {}

        def piece(self, key, chunks, cols):
            c0, c1, n0, n1 = *chunks, *cols
            i, buf = self.stage.take(sp)
            view = buf[:, 0:(c1 - c0) * (n1 - n0)].rearrange("p (c n) -> p c n", n=n1 - n0)
            hi, lo = self.hi[:, c0:c1, n0:n1], self.lo[:, c0:c1, n0:n1]
            t = load(f"stage{i}", view, self.w[c0 * P:c1 * P, self.col0 + n0:self.col0 + n1].rearrange(
                "(c p) n -> p c n", p=P))
            act.wait(t)
            th = act.do(lambda e: e.copy(hi, view), c_hi)
            dve.wait(t, th)
            tl = dve.do(lambda e: e.tensor_tensor(lo, view, raw(hi), ALU.subtract), c_wlo)
            self.stage.free(i, th, tl)
            self.ready[key] = (th, tl)

        def columns(self, m):
            self.piece(m, (0, self.chunks), (m * P, (m + 1) * P))

        def chunk(self, c):
            for n in range(0, self.cols, 512):
                self.piece(c, (c, c + 1), (n, n + 512))

    def weave(*generators):
        left = [g for g in generators if g is not None]
        while left:
            for g in list(left):
                if next(g, StopIteration) is StopIteration:
                    left.remove(g)

    def after(steps, generator):
        for _ in range(steps):
            yield
        yield from generator

    def norm_rows(x, rows, stats, mean_var, rstd, eps, xn, tiles, ready, xn_free):
        dve.wait(*ready)
        for t in tiles:
            r = rows(t)
            s = dve.do(lambda e, t=t, r=r: e.bn_stats(stats[0:r, t, :], x[0:r, t, :]), c_norm)
        dve.wait(s)
        for t in tiles:
            r = rows(t)
            s = dve.do(lambda e, t=t, r=r: e.bn_aggr(mean_var[0:r, t, :], stats[0:r, t, :]), c_norm)
        dve.wait(*xn_free)
        return scale_rows(x, rows, mean_var, rstd, eps, xn, tiles, s)

    def scale_rows(x, rows, mean_var, rstd, eps, xn, tiles, aggregated):
        ticks = []
        pool.wait(aggregated)
        k = 0
        groups = {}
        for t in tiles:
            groups.setdefault(rows(t), []).append(t)
        for r, ts in groups.items():
            t0, t1 = ts[0], ts[-1] + 1
            s = pool.do(lambda e, r=r, t0=t0, t1=t1: e.tensor_scalar(
                rstd[0:r, t0:t1], mean_var[0:r, t0:t1, 1], eps, None, ALU.add), c_rstd)
            pool.wait(s)
            s = pool.do(lambda e, r=r, t0=t0, t1=t1: e.tensor_tensor(
                rstd[0:r, t0:t1], rstd[0:r, t0:t1], minus_half[0:r, 0:t1 - t0], ALU.pow), c_rstd)
        dve.wait(s, aggregated)
        for t in tiles:
            r = rows(t)
            ticks.append(dve.do(lambda e, t=t, r=r: e.tensor_scalar(
                xn[0:r, t, :], x[0:r, t, :], mean_var[0:r, t, 0:1], rstd[0:r, t:t + 1],
                ALU.subtract, ALU.mult), c_norm))
        return ticks

    def parts_of(src, bnk_free, wide, hi, lo, produced, bias=None, scale=1.0):
        act.wait(*produced)
        kw = {} if bias is None and scale == 1.0 else {"bias": 0.0 if bias is None else bias, "scale": scale}
        fn = ACT.Copy if not kw else ACT.Identity
        wi, w = wide.take(act)
        tw = act.do(lambda e: e.activation(w[:, 0:src.shape[1]], src, fn, **kw), c_wide)
        th = act.do(lambda e: e.activation(hi, src, fn, **kw), c_hi)
        dve.wait(th)
        tl = dve.do(lambda e: e.tensor_tensor(lo, w[:, 0:src.shape[1]], raw(hi), ALU.subtract), c_lo)
        wide.free(wi, tl)
        return th, tl

    class Norm:

        def __init__(self, ctx, eps, mods, wide, psum, parts, source):
            self.eps, self.mods, self.wide, self.psum, self.source = eps, mods, wide, psum, source
            self.stats, self.mean_var = sb(ctx, "stats", [P, NT, 6]), sb(ctx, "mean_var", [P, NT, 2])
            self.rstd, self.xn = sb(ctx, "rstd", [P, NT]), sb(ctx, "x_normed", [P, NT, D])
            self.parts = parts
            self.xn_free = ()

        def batch(self, b, st):
            xn, stats, mean_var, rstd = self.xn, self.stats, self.mean_var, self.rstd
            sp.wait(*self.xn_free)
            t_x = load("x_norm", xn[:], self.source[b].rearrange("(t p) d -> p t d", p=P))
            yield
            dve.wait(t_x)
            for t in range(NT):
                s = dve.do(lambda e, t=t: e.bn_stats(stats[:, t, :], xn[:, t, :]), c_norm)
                yield
            dve.wait(s)
            for t in range(NT):
                s = dve.do(lambda e, t=t: e.bn_aggr(mean_var[:, t, :], stats[:, t, :]), c_norm)
            pool.wait(s)
            s2 = pool.do(lambda e: e.tensor_scalar(rstd[:], mean_var[:, :, 1], self.eps, None, ALU.add), c_rstd)
            pool.wait(s2)
            s2 = pool.do(lambda e: e.tensor_tensor(rstd[:], rstd[:], minus_half[:], ALU.pow), c_rstd)
            yield
            dve.wait(s, s2)
            for t in range(NT):
                ready = dve.do(lambda e, t=t: e.tensor_scalar(
                    xn[:, t, :], xn[:, t, :], mean_var[:, t, 0:1], rstd[:, t:t + 1], ALU.subtract, ALU.mult), c_norm)
                yield
            st["parts_i"], (xh, xl) = self.parts.take(act, dve)
            st["xh"], st["xl"], st["t_parts"] = xh, xl, []
            for c in range(KC):
                i, bk = self.psum.take(pe)
                pe.wait(ready)
                for t in range(NT):
                    tp = pe.do(lambda e, c=c, t=t, bk=bk: e.transpose(
                        bank[:, bk, t * P:(t + 1) * P], xn[:, t, c * P:(c + 1) * P], ident[:, :]),
                        c_turn if t == NT - 1 else None)
                kw = {}
                if self.mods:
                    sc, sh = (MODS.index(m) for m in self.mods)
                    kw = {"scale": mod_col[:, sc, c, b:b + 1], "bias": mod_col[:, sh, c, b:b + 1]}
                th, tl = parts_of(bank[:, bk, :], None, self.wide, xh[:, c, :], xl[:, c, :], (tp,), **kw)
                self.psum.free(i, th)
                st["t_parts"] += [th, tl]
                if c == KC - 1:
                    self.xn_free = (tp,)
                yield

    def product_steps(out_ap, pairs, done, at_once=3):
        terms = [(l, r) for lh, ll, rh, rl in pairs for l, r in ((lh, rh), (lh, rl), (ll, rh))]
        for k, (l, r) in enumerate(terms):
            last = k == len(terms) - 1
            tick = pe.do(lambda e, l=l, r=r, k=k, last=last: e.matmul(out_ap, l, r, start=k == 0, stop=last),
                         c_proj if last else None)
            if last:
                done.append(tick)
            elif k % at_once == at_once - 1:
                yield

    def product(out_ap, pairs):
        done = []
        weave(product_steps(out_ap, pairs, done))
        return done[0]

    with ExitStack() as ctx:
        stage_name[0] = "modulation"
        cond = sb(ctx, "cond_rows", [B, D])
        work = [sb(ctx, f"silu_{n}", [B, D]) for n in ("exp", "one_plus", "recip", "value")]
        cond_T = sb(ctx, "silu_cond_columns", [P, KC, B])
        wbuf = Ring([sb(ctx, f"mod_weights{i}", [P, KC, D]) for i in range(3)])
        bias_rows = sb(ctx, "mod_bias_rows", [B, 10, D])
        proj_bias = [sb(ctx, f"gated_bias_rows{i}", [B, D]) for i in range(2)]
        rows = sb(ctx, "modulation_rows", [B, 10, D])
        gated = sb(ctx, "gate_times_bias", [B, 2, D])
        bias_chunks = sb(ctx, "bias_chunks", [n_bias, P])

        t = pool.do(lambda e: e.memset(ident[:], 0.0), c_const)
        pool.do(lambda e: e.memset(ones[:], 1.0), c_const)
        pool.do(lambda e: e.memset(minus_half[:], -0.5), c_const)
        pool.wait(t)
        const = pool.do(lambda e: e.affine_select(
            out=ident[:], in_=ident[:], compare_op=ALU.not_equal, fill=1.0, base=0,
            pattern=[[-1, P]], channel_multiplier=1), c_const)

        t_cond = load("cond", cond[:], a["cond_1024"])
        sources = [("L0_xcond_Wss_q", "L0_xcond_bss_q", 0), ("L0_xcond_Wss_q", "L0_xcond_bss_q", 1),
                   ("L0_xcond_Wss_kv", "L0_xcond_bss_kv", 0), ("L0_xcond_Wss_kv", "L0_xcond_bss_kv", 1)]
        sources += [("L1_xcond_W_mod", "L1_xcond_b_mod", j) for j in range(6)]
        names = MODS[0:4] + ["a_shift", "a_scale", "a_gate", "m_shift", "m_scale", "m_gate"]
        for j, (_, bname, part) in enumerate(sources):
            t_bias = load("mod_bias", bias_rows[:, j, :],
                          a[bname][part * D:(part + 1) * D].partition_broadcast(B))
        for i, bname in enumerate(("L1_xcond_b_proj", "L1_xcond_b_mlp2")):
            t_bias = load("mod_bias", proj_bias[i][:], a[bname].partition_broadcast(B))
        at = 0
        for bname, n in BIAS_COLS:
            full = bname.replace("_", "_xcond_", 1)
            bias_col[bname] = at
            t_cols = load("bias_chunks", bias_chunks[at:at + n // P, :], a[full][0:n].rearrange("(c p) -> c p", p=P))
            at += n // P

        act.wait(t_cond)
        t = act.do(lambda e: e.activation(work[0][:], cond[:], ACT.Exp, scale=-1.0), c_exp)
        dve.wait(t)
        t = dve.do(lambda e: e.tensor_scalar(work[1][:], work[0][:], 1.0, None, ALU.add), c_norm)
        dve.wait(t)
        t = dve.do(lambda e: e.reciprocal(work[2][:], work[1][:]), c_norm)
        dve.wait(t)
        t = dve.do(lambda e: e.tensor_tensor(work[3][:], cond[:], work[2][:], ALU.mult), c_norm)
        pe.wait(t, const)
        for c in range(KC):
            t = pe.do(lambda e, c=c: e.transpose(bank[:, 7, c * B:(c + 1) * B], work[3][:, c * P:(c + 1) * P],
                                                 ident[0:B, 0:B]), c_turn)
        dve.wait(t)
        t_condT = dve.do(lambda e: e.tensor_copy(cond_T[:], bank[:, 7, 0:KC * B].rearrange("p (c b) -> p c b", b=B)), c_norm)

        pe.wait(t_cols)
        t = pe.do(lambda e: e.transpose(bank[:, 6, 0:n_bias], bias_chunks[:], ident[0:n_bias, 0:n_bias]), c_turn)
        act.wait(t)
        act.do(lambda e: e.copy(bias_cols[:], bank[:, 6, 0:n_bias]), c_wide)

        psum = Ring([0, 1, 2])
        turned = Ring([4, 5])
        for j, (wname, _, part) in enumerate(sources):
            i, w = wbuf.take(sp)
            t_w = load(f"mod_w{i}", w[:], a[wname][:, part * D:(part + 1) * D].rearrange("(c p) n -> p c n", p=P))
            bi, bk = psum.take(pe)
            pe.wait(t_w, t_condT)
            for c in range(KC):
                t = pe.do(lambda e, c=c, w=w, bk=bk: e.matmul(bank[0:B, bk, :], cond_T[:, c, :], w[:, c, :],
                                                             start=c == 0, stop=c == KC - 1), c_proj)
            wbuf.free(i, t)
            dve.wait(t, t_bias)
            one = 1.0 if names[j].endswith("scale") else 0.0
            t = dve.do(lambda e, j=j, bk=bk, one=one: e.scalar_tensor_tensor(
                rows[:, j, :], bank[0:B, bk, :], one, bias_rows[:, j, :], ALU.add, ALU.add), c_norm)
            psum.free(bi, t)
            if names[j].endswith("gate"):
                g = 0 if names[j] == "a_gate" else 1
                t_r = t
                dve.wait(t)
                t = dve.do(lambda e, j=j, g=g: e.tensor_tensor(gated[:, g, :], rows[:, j, :], proj_bias[g][:], ALU.mult), c_norm)
                sp.wait(t_r, t)
                load("gates_out", gate_rows[g, 0], rows[:, j, :])
                load("gates_out", gate_rows[g, 1], gated[:, g, :])
            else:
                m = MODS.index(names[j])
                ti, tb = turned.take(pe)
                pe.wait(t)
                for c in range(KC):
                    t = pe.do(lambda e, c=c, j=j, tb=tb: e.transpose(
                        bank[:, tb, c * B:(c + 1) * B], rows[:, j, c * P:(c + 1) * P], ident[0:B, 0:B]), c_turn)
                dve.wait(t)
                t = dve.do(lambda e, m=m, tb=tb: e.tensor_copy(
                    mod_col[:, m, :, :], bank[:, tb, 0:KC * B].rearrange("p (c b) -> p c b", b=B)), c_norm)
                turned.free(ti, t)
        block()

    with ExitStack() as ctx:
        stage_name[0] = "context"
        CT = B * S
        HALF = CT // 2
        TT = -(-CT // P)
        rows_of = lambda t: min(P, CT - t * P)
        stage = Ring([sb(ctx, f"weight_stage{i}", [P, 1024]) for i in range(2)])
        xc = sb(ctx, "context_rows", [P, TT, D])
        stats, mean_var = sb(ctx, "stats", [P, TT, 6]), sb(ctx, "mean_var", [P, TT, 2])
        rstd = sb(ctx, "rstd", [P, TT])
        xn = sb(ctx, "context_normed", [P, TT, D])
        xT = sb(ctx, "context_turned", [P, KC, CT])
        xh, xl = sb(ctx, "context_hi", [P, KC, CT], F32R), sb(ctx, "context_lo", [P, KC, CT], F32R)
        wide = Ring([sb(ctx, f"wide{i}", [P, 512]) for i in range(2)])
        kst = Ring([sb(ctx, f"key_parts{i}", [P, 2, HALF], F32R) for i in range(2)])
        vst = Ring([sb(ctx, f"value_rows{i}", [S, D]) for i in range(2)])
        bv = [sb(ctx, f"value_bias{l}", [S, D]) for l in (0, 1)]
        flat = a["ctx_1024"].rearrange("b s d -> (b s) d")
        full = CT // P
        load("ctx", xc[:, 0:full, :], flat[0:full * P].rearrange("(t p) d -> p t d", p=P))
        t_x = load("ctx", xc[0:CT - full * P, full, :], flat[full * P:CT])
        wkv = ["L0_xcond_Wkv", "L1_xcond_W_kvc"]
        bkv = ["L0_xcond_bkv", "L1_xcond_b_kvc"]
        for l in (0, 1):
            t_bv = load("value_bias", bv[l][:], a[bkv[l]][D:2 * D].partition_broadcast(S))
        weights = [Weights(ctx, f"w_kv{l}", a[wkv[l]], 0, 2 * D, stage) for l in (0, 1)]
        psum, proj = Ring([0, 1, 2]), Ring([3, 4, 5])
        parts_free = ()
        xT_free = ()
        xn_free = ()
        for l, eps in ((0, 1e-5), (1, 1e-6)):
            if l == 0:
                ready = norm_rows(xc, rows_of, stats, mean_var, rstd, eps, xn, range(TT), (t_x,), ())
            else:
                dve.wait(*xn_free)
                pool.wait(ready[-1])
                ready = scale_rows(xc, rows_of, mean_var, rstd, eps, xn, range(TT), ready[-1])
            pe.wait(ready[-1])
            for c in range(KC):
                for t0, t1 in ((0, 4), (4, TT)):
                    bi, bk = psum.take(pe)
                    w_ = sum(rows_of(t) for t in range(t0, t1))
                    for t in range(t0, t1):
                        r = rows_of(t)
                        tp = pe.do(lambda e, c=c, t=t, r=r, bk=bk, t0=t0: e.transpose(
                            bank[:, bk, (t - t0) * P:(t - t0) * P + r], xn[0:r, t, c * P:(c + 1) * P],
                            ident[0:r, 0:r]), c_turn)
                    act.wait(tp, *xT_free)
                    tw = act.do(lambda e, c=c, t0=t0, w_=w_, bk=bk: e.activation(
                        xT[:, c, t0 * P:t0 * P + w_], bank[:, bk, 0:w_], ACT.Copy), c_wide)
                    psum.free(bi, tw)
            xn_free = (tp,)
            act.wait(tw)
            if l == 0:
                for c in range(KC):
                    for b in range(B):
                        tw = act.do(lambda e, c=c, b=b: e.activation(
                            xT[:, c, b * S:(b + 1) * S], xT[:, c, b * S:(b + 1) * S], ACT.Identity,
                            bias=mod_col[:, 3, c, b:b + 1], scale=mod_col[:, 2, c, b:b + 1]), c_wide)
                act.wait(tw)
            for c in range(KC):
                act.wait(*parts_free)
                th = act.do(lambda e, c=c: e.copy(xh[:, c, :], xT[:, c, :]), c_hi)
                dve.wait(th, *parts_free)
                tl = dve.do(lambda e, c=c: e.tensor_tensor(xl[:, c, :], xT[:, c, :], raw(xh[:, c, :]), ALU.subtract), c_lo)
            xT_free = (tl,)
            wl_ = weights[l]
            wh, wl = wl_.hi, wl_.lo
            for m in range(G):
                wl_.columns(m)
            pe.wait(th, tl)
            bcol = bias_col["L0_bkv" if l == 0 else "L1_b_kvc"]
            for g in range(G):
                pe.wait(*wl_.ready[g])
                wl_.columns(G + g)
                for h in range(2):
                    bi, bk = proj.take(pe)
                    cols = slice(h * HALF, (h + 1) * HALF)
                    f = slice(g * P, (g + 1) * P)
                    tp = product(bank[:, bk, 0:HALF], [(wh[:, c, f], wl[:, c, f], xh[:, c, cols], xl[:, c, cols])
                                                      for c in range(KC)])
                    ki, kt = kst.take(act, dve)
                    th, tl = parts_of(bank[:, bk, 0:HALF], None, wide, kt[:, 0, :], kt[:, 1, :], (tp,),
                                      bias=bias_cols[:, bcol + g:bcol + g + 1])
                    proj.free(bi, th)
                    sp.wait(th, tl)
                    t = load(f"key_store{ki}", k_ctx[l][:, f, cols].rearrange("s p t -> p s t"), raw(kt[:]))
                    kst.free(ki, t)
            pe.wait(*(t for g in range(G) for t in wl_.ready[G + g]))
            for b in range(B):
                bi, bk = proj.take(pe)
                r = slice(b * S, (b + 1) * S)
                tp = product(bank[0:S, bk, :], [(xh[:, c, r], xl[:, c, r], wh[:, c, D:2 * D], wl[:, c, D:2 * D])
                                               for c in range(KC)])
                vi, vt = vst.take(dve)
                dve.wait(tp, t_bv)
                t = dve.do(lambda e, bk=bk, l=l, vt=vt: e.tensor_tensor(vt[:], bank[0:S, bk, :], bv[l][:], ALU.add), c_res)
                proj.free(bi, t)
                sp.wait(t)
                vst.free(vi, load(f"value_store{vi}", v_ctx[l][b], vt[:]))
            parts_free = (tp,)
        block()

    def attention_stage(name, x_in, x_out, wq, bq, wp, bp, mods, eps, layer):
        own_q = layer is not None
        keys = S if own_q else P
        KT = 1 if own_q else NT
        with ExitStack() as ctx:
            stage_name[0] = name
            x_ring = Ring([sb(ctx, "x_rows", [P, NT, D])])
            PL = 3
            QUERY, FETCH, MAX, ROWS = (5, 4, 3, 2) if own_q else (4, 3, 2, 1)
            q_ring = Ring([sb(ctx, f"query_stack{i}", [ST_MAX, GH, N], F32R) for i in range(FETCH + 1)])
            if own_q:
                k_ring = Ring([sb(ctx, f"key_stack{i}", [ST_MAX, NH, SP_], F32R) for i in range(2)])
            else:
                k_ring = Ring([sb(ctx, f"key_stack{i}", [ST_MAX, GH, N], F32R) for i in range(4)])
            v_ring = Ring([sb(ctx, f"values{i}", [keys, KT, D]) for i in range(2)])
            p_ring = Ring([sb(ctx, f"exponentials{i}", [keys, GH, N]) for i in range(2 if own_q else 4)])
            o_ring = Ring([(sb(ctx, f"heads_hi{i}", [P, G, N], F32R), sb(ctx, f"heads_lo{i}", [P, G, N], F32R))
                           for i in range(2)])
            sums_turned = sb(ctx, "sums_turned", [P, N])
            recip_turned = sb(ctx, "reciprocals_turned", [P, N // HD])
            recip = sb(ctx, "reciprocal_sums", [P, N])
            o_wide = Ring([sb(ctx, f"heads_float32_{i}", [P, N]) for i in range(2)])
            negmax = Ring([sb(ctx, f"negated_max{i}", [P, GH * NT]) for i in range(2)])
            max_rows = Ring([sb(ctx, f"max_row_parts{i}", [GH * NT, 2, P], F32R) for i in range(2)])
            for i, k in enumerate(k_ring.slots):
                if own_q:
                    dve.do(lambda e, k=k: e.memset(raw(k[0:ST]), 0.0), c_vconst)
                t_ones = dve.do(lambda e, k=k: e.memset(raw(k[ST:ST_MAX]), 1.0), c_vconst)
                k_ring.free(i, t_ones)
            stage = Ring([sb(ctx, f"weight_stage{i}", [P, 512]) for i in range(2)])
            work, heads, sums = Ring(range(6)), Ring([6]), Ring([7])
            smax = score = work
            if own_q:
                wide = Ring([sb(ctx, f"wide{i}", [P, N]) for i in range(2)])
                parts = Ring([(sb(ctx, "x_hi", [P, KC, N], F32R), sb(ctx, "x_lo", [P, KC, N], F32R))])
                norm = Norm(ctx, eps, mods, wide, work, parts, x_in)
                q_out = Ring([sb(ctx, f"query_parts{i}", [P, 2, N], F32R) for i in range(2)])
                w_q = Weights(ctx, "w_q", wq, 0, D, stage)
                bias_tile = sb(ctx, "projection_bias", [P, D])
                t_bias = load("projection_bias", bias_tile[:], bp.partition_broadcast(P))
            else:
                gate = Ring([sb(ctx, f"gate_and_bias{i}", [P, 2, D]) for i in range(2)])
                gated_rows = Ring([sb(ctx, f"gated_rows{i}", [P, D]) for i in range(2)])
            w_p = Weights(ctx, "w_proj", wp, 0, D, stage)
            batch = [{} for _ in range(B)]
            group = {(b, g): {} for b in range(B) for g in range(G)}

            def load_keys(b):
                if own_q:
                    st = batch[b]
                    st["ki"], st["k"] = k_ring.take(sp)
                    src = k_ctx[layer][:, :, b * S:(b + 1) * S].rearrange("s (h p) t -> s p h t", p=HD)
                    for r, s in ((0, 0), (1, 0), (2, 1)):
                        st["t_k"] = load(f"k{st['ki']}", raw(st["k"][r * HD:(r + 1) * HD, :, 0:S]), src[s])

            def load_values(b):
                st = batch[b]
                st["vi"], st["v"] = v_ring.take(sp)
                src = v_ctx[layer][b].unsqueeze(1) if own_q else v_self[b].rearrange("(t p) d -> p t d", p=P)
                st["t_v"] = load(f"v{st['vi']}", st["v"][:], src)

            def load_base(b):
                st = batch[b]
                st["xi"], st["x"] = x_ring.take(sp)
                st["t_x"] = load("x_rows", st["x"][:], x_in[b].rearrange("(t p) d -> p t d", p=P))
                if not own_q:
                    st["gi"], st["gate"] = gate.take(sp)
                    for w in range(2):
                        st["t_gate"] = load(f"gate{st['gi']}", st["gate"][:, w, :],
                                            gate_rows[0, w, b].partition_broadcast(P))

            def add_base(b):
                st = batch[b]
                rhs, t_rhs = (bias_tile[:], t_bias) if own_q else (st["gate"][:, 1, :], st["t_gate"])
                pool.wait(st["t_x"], t_rhs)
                st["t_base"] = [pool.do(lambda e, t=t: e.tensor_tensor(
                    st["x"][:, t, :], st["x"][:, t, :], rhs, ALU.add), c_xb) for t in range(NT)]

            def query(b, g):
                st = batch[b]
                xh, xl, hi, lo = st["xh"], st["xl"], w_q.hi, w_q.lo
                pi, bk = work.take(pe)
                pe.wait(*w_q.ready[g])
                pe.wait(*st["t_parts"])
                f = slice(g * P, (g + 1) * P)
                done = []
                yield from product_steps(bank[:, bk, :], [(hi[:, c, f], lo[:, c, f], xh[:, c, :], xl[:, c, :]) for c in range(KC)], done)
                tp = done[0]
                if g == G - 1:
                    parts.free(st["parts_i"], tp)
                qi, qt = q_out.take(act, dve)
                th, tl = parts_of(bank[:, bk, :], None, wide, qt[:, 0, :], qt[:, 1, :], (tp,),
                                  bias=bias_cols[:, bias_col[bq] + g:bias_col[bq] + g + 1])
                work.free(pi, th)
                sp.wait(th, tl)
                t = store_parts(f"q_store{qi}", q_parts[name][b, g], qt)
                q_out.free(qi, t)
                group[b, g]["stored"] = t
                yield

            def fetch(b, g):
                gr = group[b, g]
                sp.wait(gr.get("stored"))
                gr["qi"], gr["q"] = q_ring.take(sp)
                src = q_parts[name][b, g].rearrange("s p h t -> (s p) (h t)")
                stack = raw(gr["q"][:]).rearrange("r h t -> r (h t)")
                load(f"q{gr['qi']}", stack[0:2 * HD], src)
                gr["t_q"] = load(f"q{gr['qi']}", stack[2 * HD:ST], src[0:HD])
                if own_q:
                    gr["k"] = batch[b]["k"][:, g * GH:(g + 1) * GH, :]
                    gr["t_k"] = batch[b]["t_k"]
                else:
                    gr["ki"], gr["k"] = k_ring.take(sp)
                    src = k_self[b, g].rearrange("s p h t -> (s p) (h t)")
                    stack = raw(gr["k"][:]).rearrange("r h t -> r (h t)")
                    load(f"k{gr['ki']}", stack[0:HD], src[0:HD])
                    gr["t_k"] = load(f"k{gr['ki']}", stack[HD:ST], src)

            def maxima(b, g):
                gr = group[b, g]
                ni, nm = negmax.take(dve)
                pe.wait(gr["t_q"], gr["t_k"])
                for qt in range(NT):
                    rows = slice(qt * P, (qt + 1) * P)
                    if own_q:
                        si, bk = smax.take(pe)
                        for h in range(GH):
                            tp = pe.do(lambda e, h=h, bk=bk, rows=rows: e.matmul(
                                bank[:, bk, h * SP_:(h + 1) * SP_], gr["q"][0:ST, h, rows], gr["k"][0:ST, h, :],
                                start=True, stop=True), c_smax)
                        dve.wait(tp)
                        tn = dve.do(lambda e, bk=bk, qt=qt: e.tensor_reduce(
                            nm[:, qt:GH * NT:NT], bank[:, bk, 0:GH * SP_].rearrange("p (h k) -> p h k", k=SP_)[:, :, 0:S],
                            AX_X, ALU.max, negate=True), c_negmax)
                        smax.free(si, tn)
                        yield
                    else:
                        for h in range(GH):
                            si, bk = smax.take(pe)
                            tp = pe.do(lambda e, h=h, bk=bk, rows=rows: e.matmul(
                                bank[:, bk, :], gr["q"][0:ST, h, rows], gr["k"][0:ST, h, :],
                                start=True, stop=True), c_smax)
                            dve.wait(tp)
                            tn = dve.do(lambda e, bk=bk, qt=qt, h=h: e.tensor_reduce(
                                nm[:, h * NT + qt:h * NT + qt + 1], bank[:, bk, :], AX_X, ALU.max, negate=True), c_negmax)
                            smax.free(si, tn)
                            yield
                gr["negmax"] = (ni, nm, tn)

            def max_rows_of(b, g):
                gr = group[b, g]
                ni, nm, tn = gr["negmax"]
                si, bk = smax.take(pe)
                pe.wait(tn)
                tp = pe.do(lambda e: e.transpose(bank[0:GH * NT, bk, 0:P], nm[:], ident[:]), c_turn)
                negmax.free(ni, tp)
                mi, mr = max_rows.take(act, dve)
                act.wait(tp)
                th = act.do(lambda e: e.activation(mr[:, 0, :], bank[0:GH * NT, bk, 0:P], ACT.Copy), c_hi)
                dve.wait(th)
                tl = dve.do(lambda e: e.tensor_tensor(mr[:, 1, :], bank[0:GH * NT, bk, 0:P], raw(mr[:, 0, :]), ALU.subtract), c_lo)
                smax.free(si, tl)
                sp.wait(th, tl, tp)
                for w in range(2):
                    gr["t_max"] = load(f"max{gr['qi']}", raw(gr["q"][ST + w:ST + w + 1].rearrange("a h (t q) -> a (h t) q", q=P)),
                                       raw(mr[:, w, :]))
                max_rows.free(mi, gr["t_max"])
                yield

            late = []

            def attend(b, g):
                gr, st = group[b, g], batch[b]
                pe.wait(gr["t_max"])
                for kt in range(KT):
                    pi, pt = p_ring.take(act)
                    cols = slice(kt * P, kt * P + keys)
                    for h in range(GH):
                        si, bk = score.take(pe)
                        tp = pe.do(lambda e, h=h, bk=bk, cols=cols: e.matmul(
                            bank[0:keys, bk, :], gr["k"][0:ST_MAX, h, cols], gr["q"][0:ST_MAX, h, :],
                            start=True, stop=True), c_score)
                        act.wait(tp)
                        te = act.do(lambda e, h=h, bk=bk, pt=pt: e.activation(
                            pt[:, h, :], bank[0:keys, bk, :], ACT.Exp, scale=SCALE), c_exp)
                        score.free(si, te)
                        yield
                        if h == (0 if own_q else 1):
                            while late:
                                values(*late.pop(0))
                    if kt == KT - 1:
                        q_ring.free(gr["qi"], tp)
                        if not own_q:
                            k_ring.free(gr["ki"], tp)
                        elif g == G - 1:
                            k_ring.free(st["ki"], tp)
                    late.append((b, g, kt, pi, pt, te))

            def values(b, g, kt, pi, pt, te):
                st, gr = batch[b], group[b, g]
                if kt == 0:
                    gr["heads"], gr["sums"] = heads.take(pe)[1], sums.take(pe)[1]
                pe.wait(te, st["t_v"])
                for ones_turn in (False, True):
                    bk = gr["sums"] if ones_turn else gr["heads"]
                    for h in range(GH):
                        f = (g * GH + h) * HD
                        w = ones[0:keys, :] if ones_turn else st["v"][:, kt, f:f + HD]
                        tp = pe.do(lambda e, h=h, bk=bk, w=w: e.matmul(
                            bank[h * HD:(h + 1) * HD, bk, :], w, pt[:, h, :],
                            start=kt == 0, stop=kt == KT - 1), c_av)
                p_ring.free(pi, tp)
                if kt == KT - 1:
                    gr["t_values"] = tp
                    if g == G - 1:
                        v_ring.free(st["vi"], tp)

            def finish(b, g):
                gr, st = group[b, g], batch[b]
                while "t_values" not in gr:
                    yield
                if g == 0:
                    st["oi"], st["o"] = o_ring.take(act, dve)
                wi, w = o_wide.take(act)
                act.wait(gr["t_values"])
                th = act.do(lambda e: e.copy(w[:], bank[:, gr["heads"], :]), c_wide)
                heads.free(0, th)
                dve.wait(gr["t_values"])
                t = dve.do(lambda e: e.transpose(sums_turned[:], bank[:, gr["sums"], :]), c_out)
                sums.free(0, t)
                yield
                dve.wait(t)
                t = dve.do(lambda e: e.reciprocal(recip_turned[:], sums_turned[:, 0:N:HD]), c_out)
                yield
                dve.wait(t)
                t = dve.do(lambda e: e.transpose(
                    recip[:].rearrange("p (a b) -> p a b", b=HD),
                    recip_turned[:].unsqueeze(2).broadcast_to([P, N // HD, HD])), c_out)
                yield
                dve.wait(t, th)
                to = dve.do(lambda e: e.tensor_tensor(w[:], w[:], recip[:], ALU.mult), c_out)
                oh, ol = st["o"]
                yield
                act.wait(to)
                th = act.do(lambda e: e.copy(oh[:, g, :], w[:]), c_hi)
                yield
                dve.wait(th)
                tl = dve.do(lambda e: e.tensor_tensor(ol[:, g, :], w[:], raw(oh[:, g, :]), ALU.subtract), c_lo)
                o_wide.free(wi, tl)
                st["t_o"] = (th, tl)

            def project(b):
                st = batch[b]
                oh, ol = st["o"]
                for t in range(NT):
                    pe.wait(*st["t_o"], *(x for c in range(KC) for x in w_p.ready[c]))
                    pi, bk = work.take(pe)
                    r = slice(t * P, (t + 1) * P)
                    done = []
                    yield from product_steps(bank[:, bk, :], [(oh[:, c, r], ol[:, c, r], w_p.hi[:, c, :], w_p.lo[:, c, :]) for c in range(KC)], done)
                    tp = done[0]
                    dve.wait(tp, st["t_base"][t])
                    if own_q:
                        tres = dve.do(lambda e, t=t, bk=bk: e.tensor_tensor(
                            st["x"][:, t, :], bank[:, bk, :], st["x"][:, t, :], ALU.add), c_res)
                        work.free(pi, tres)
                    else:
                        dve.wait(st["t_gate"])
                        wi, w = gated_rows.take(dve)
                        tg = dve.do(lambda e, bk=bk, w=w: e.tensor_tensor(w[:], bank[:, bk, :], st["gate"][:, 0, :], ALU.mult), c_res)
                        work.free(pi, tg)
                        dve.wait(tg)
                        tres = dve.do(lambda e, t=t, w=w: e.tensor_tensor(
                            st["x"][:, t, :], w[:], st["x"][:, t, :], ALU.add), c_res)
                        gated_rows.free(wi, tres)
                    if t == NT - 1:
                        o_ring.free(st["oi"], tp)
                        if not own_q:
                            gate.free(st["gi"], tres)
                        sp.wait(tres)
                        x_ring.free(st["xi"], load("x_out", x_out[b].rearrange("(t p) d -> p t d", p=P), st["x"][:]))
                    yield

            seq = [(b, g) for b in range(B) for g in range(G)]
            last = len(seq)

            def of_group(make, n):
                return make(*seq[n]) if n < last else iter(())

            def norm_quarter(n):
                b, g = seq[n][0] + 1, seq[n][1]
                if b == B:
                    return None
                if g == 0:
                    batch[b]["turning"] = norm.batch(b, batch[b])
                    next(batch[b]["turning"])
                turning = batch[b]["turning"]
                if g == 1:
                    return (next(turning) for _ in range(NT + 1))
                if g == 2:
                    return after(1, (next(turning) for _ in range(NT)))
                return after(2, turning) if g == 3 else None

            load_keys(0)
            load_values(0)
            if own_q:
                turning = norm.batch(0, batch[0])
                next(turning)
                w_q.columns(0)
                w_q.columns(1)
                weave(turning)
                for n in range(QUERY):
                    if n + 2 < G:
                        w_q.columns(n + 2)
                    asking = query(*seq[n])
                    weave(asking, asking, norm_quarter(n))
                    if n < FETCH:
                        fetch(*seq[n])
            else:
                for n in range(FETCH):
                    fetch(*seq[n])
            for n in range(MAX):
                weave(maxima(*seq[n]), max_rows_of(*seq[n - 1]) if n and n - 1 < ROWS else None)
            for n, (b, g) in enumerate(seq):
                if n < G:
                    w_p.chunk(n)
                if g == 0 and b + 1 < B:
                    load_keys(b + 1)
                if n + FETCH < last:
                    fetch(*seq[n + FETCH])
                side = []
                if g == 1 and b > 0:
                    add_base(b - 1)
                    projecting = project(b - 1)
                if g > 0 and b > 0:
                    tiles = (0, 1, 2, 1)[g]
                    part = after(PL if g == 1 else 0, (next(projecting) for _ in range(tiles * KC)))
                    side += [part] * tiles
                asking = of_group(query, n + QUERY) if own_q else None
                quarter = (g + QUERY) % G
                if own_q and quarter == 0:
                    asking = after(2, asking)
                weave(attend(b, g),
                      asking, asking if quarter == G - 1 else None,
                      after(2 if own_q else 0, of_group(maxima, n + MAX)),
                      after(2, of_group(max_rows_of, n + ROWS)),
                      finish(*seq[n - 1]) if n else None,
                      norm_quarter(n + QUERY) if own_q and n + QUERY < last else None,
                      *side)
                if g == 0 and b + 1 < B:
                    load_values(b + 1)
                if g == 0 and b > 0:
                    load_base(b - 1)
            while late:
                values(*late.pop(0))
            load_base(B - 1)
            weave(finish(*seq[-1]))
            add_base(B - 1)
            weave(project(B - 1))
            block()

    attention_stage("L0", a["x"], x1, a["L0_xcond_Wq"], "L0_bq", a["L0_xcond_Wp"], a["L0_xcond_bp"],
                    ("L0q_scale", "L0q_shift"), 1e-5, 0)

    with ExitStack() as ctx:
        stage_name[0] = "qkv"
        AHEAD = 4
        x_ring = Ring([sb(ctx, f"x_rows{i}", [P, NT, D]) for i in range(2)])
        stage = Ring([sb(ctx, f"weight_stage{i}", [P, 512]) for i in range(AHEAD)])
        wide = Ring([sb(ctx, f"wide{i}", [P, N]) for i in range(2)])
        parts = Ring([(sb(ctx, f"x_hi{i}", [P, KC, N], F32R), sb(ctx, f"x_lo{i}", [P, KC, N], F32R)) for i in range(2)])
        turn = proj = Ring(range(8))
        norm = Norm(ctx, 1e-6, ("a_scale", "a_shift"), wide, turn, parts, x1)
        o_parts = Ring([sb(ctx, f"qk_parts{i}", [P, 2, N], F32R) for i in range(3)])
        v_rows = Ring([sb(ctx, f"value_rows{i}", [P, D]) for i in range(3)])
        bias_tile = sb(ctx, "value_bias_tile", [P, D])
        w_qkv = Weights(ctx, "w_qkv", a["L1_xcond_W_qkv"], 0, 3 * D, stage)
        w_hi, w_lo = w_qkv.hi, w_qkv.lo
        batch = [{} for _ in range(B)]
        turning = norm.batch(0, batch[0])
        next(turning)
        for m in range(AHEAD):
            w_qkv.columns(m)
        weave(turning)
        t_bias = load("value_bias", bias_tile[:], a["L1_xcond_b_qkv"][2 * D:3 * D].partition_broadcast(P))
        for b in range(B):
            xh, xl = batch[b]["xh"], batch[b]["xl"]
            turning = norm.batch(b + 1, batch[b + 1]) if b + 1 < B else iter(())
            pe.wait(*batch[b]["t_parts"])
            for m in range(2 * G):
                if b == 0:
                    w_qkv.columns(m + AHEAD)
                pe.wait(*w_qkv.ready[m])
                pi, bk = proj.take(pe)
                f = slice(m * P, (m + 1) * P)
                tp = product(bank[:, bk, :], [(w_hi[:, c, f], w_lo[:, c, f], xh[:, c, :], xl[:, c, :]) for c in range(KC)])
                oi, ot = o_parts.take(act, dve)
                col = bias_col["L1_b_qkv"] + m
                th, tl = parts_of(bank[:, bk, :], None, wide, ot[:, 0, :], ot[:, 1, :], (tp,), bias=bias_cols[:, col:col + 1])
                proj.free(pi, th)
                sp.wait(th, tl)
                dst = q_parts["self"] if m < G else k_self
                o_parts.free(oi, store_parts(f"qk_store{oi}", dst[b, m % G], ot))
                if m != 5:
                    next(turning, None)
                if m < 4:
                    next(turning, None)
            pe.wait(*(t for m in range(2 * G, 3 * G) for t in w_qkv.ready[m]))
            for t in range(NT):
                pi, bk = proj.take(pe)
                r = slice(t * P, (t + 1) * P)
                tp = product(bank[:, bk, :], [(xh[:, c, r], xl[:, c, r], w_hi[:, c, 2 * D:3 * D], w_lo[:, c, 2 * D:3 * D])
                                              for c in range(KC)])
                vi, vt = v_rows.take(dve)
                dve.wait(tp, t_bias)
                tv = dve.do(lambda e, bk=bk, vt=vt: e.tensor_tensor(vt[:], bank[:, bk, :], bias_tile[:], ALU.add), c_res)
                proj.free(pi, tv)
                sp.wait(tv)
                v_rows.free(vi, load(f"value_store{vi}", v_self[b, r, :], vt[:]))
                next(turning, None)
            parts.free(batch[b]["parts_i"], tp)
            weave(turning)
        block()

    attention_stage("self", x1, x2, None, None, a["L1_xcond_W_proj"], None, None, None, None)
    attention_stage("cross", x2, x3, a["L1_xcond_W_qc"], "L1_b_qc", a["L1_xcond_W_cproj"], a["L1_xcond_b_cproj"],
                    None, 1e-6, 1)

    with ExitStack() as ctx:
        stage_name[0] = "mlp"
        NS = 3
        JC = HID // P
        LAG = 2
        x_rows = sb(ctx, "x_rows", [P, NT, D])
        stage = Ring([sb(ctx, f"weight_stage{i}", [P, 512]) for i in range(NS)])
        wide = Ring([sb(ctx, f"wide{i}", [P, N]) for i in range(2)])
        parts = Ring([(sb(ctx, f"x_hi{i}", [P, KC, N], F32R), sb(ctx, f"x_lo{i}", [P, KC, N], F32R)) for i in range(2)])
        acc = [4, 5, 6, 7]
        up = turn = Ring(range(4))
        norm = Norm(ctx, 1e-6, ("m_scale", "m_shift"), wide, turn, parts, x3)
        h_parts = Ring([sb(ctx, f"hidden_parts{i}", [P, 2, N], F32R) for i in range(LAG + 1)])
        gt = sb(ctx, "gate_and_bias", [P, 2, D])
        gated = Ring([sb(ctx, "gated_rows", [P, D])])
        w1 = Weights(ctx, "w_mlp1", a["L1_xcond_W_mlp1"], 0, HID, stage)
        w2 = Weights(ctx, "w_mlp2", a["L1_xcond_W_mlp2"], 0, D, stage)
        acc_free = [()] * NT
        rows_free = ()
        batch = [{} for _ in range(B)]
        turning = norm.batch(0, batch[0])
        next(turning)
        AHEAD = 3
        for j in range(AHEAD):
            w1.columns(j)
        weave(turning)

        def down(j, hi_, ht, ticks):
            pe.wait(*ticks, *w2.ready[j])
            for t in range(NT):
                if j == 0:
                    pe.wait(*acc_free[t])
                r = slice(t * P, (t + 1) * P)
                terms = [(ht[:, 0, r], w2.hi[:, j, :]), (ht[:, 0, r], w2.lo[:, j, :]), (ht[:, 1, r], w2.hi[:, j, :])]
                for k, (l, w) in enumerate(terms):
                    tick = pe.do(lambda e, l=l, w=w, k=k, t=t: e.matmul(
                        bank[:, acc[t], :], l, w, start=j == 0 and k == 0, stop=j == JC - 1 and k == 2), c_proj)
            h_parts.free(hi_, tick)
            return tick

        for b in range(B):
            xh, xl = batch[b]["xh"], batch[b]["xl"]
            turning = norm.batch(b + 1, batch[b + 1]) if b + 1 < B else iter(())
            next(turning, None)
            sp.wait(*rows_free)
            t_x = load("x_rows", x_rows[:], x3[b].rearrange("(t p) d -> p t d", p=P))
            for w in range(2):
                t_g = load("mlp_gate", gt[:, w, :], gate_rows[1, w, b].partition_broadcast(P))
            pe.wait(*batch[b]["t_parts"])
            pending = []
            for j in range(JC):
                if b == 0:
                    w2.chunk(j)
                    if j + AHEAD < JC:
                        w1.columns(j + AHEAD)
                pe.wait(*w1.ready[j])
                ui, bk = up.take(pe)
                f = slice(j * P, (j + 1) * P)
                tp = product(bank[:, bk, :], [(w1.hi[:, c, f], w1.lo[:, c, f], xh[:, c, :], xl[:, c, :]) for c in range(KC)])
                wi, w = wide.take(act)
                hi_, ht = h_parts.take(act, dve)
                act.wait(tp)
                col = bias_col["L1_b_mlp1"] + j
                tw = act.do(lambda e, w=w, bk=bk, col=col: e.activation(w[:], bank[:, bk, :], ACT.Gelu_apprx_tanh,
                                                               bias=bias_cols[:, col:col + 1]), c_wide)
                up.free(ui, tw)
                act.wait(tw)
                th = act.do(lambda e, w=w, ht=ht: e.copy(ht[:, 0, :], w[:]), c_hi)
                dve.wait(th)
                tl = dve.do(lambda e, w=w, ht=ht: e.tensor_tensor(ht[:, 1, :], w[:], raw(ht[:, 0, :]), ALU.subtract), c_lo)
                wide.free(wi, tl)
                pending.append((j, hi_, ht, (th, tl)))
                if len(pending) == LAG:
                    down(*pending.pop(0))
                if j > 0 and j != 6:
                    next(turning, None)
                if j == 8:
                    pool.wait(t_x, t_g)
                    for t in range(NT):
                        t_base = pool.do(lambda e, t=t: e.tensor_tensor(
                            x_rows[:, t, :], x_rows[:, t, :], gt[:, 1, :], ALU.add), c_xb)
            parts.free(batch[b]["parts_i"], tp)
            weave(turning)
            for item in pending:
                tick = down(*item)
            for t in range(NT):
                pi, pr = gated.take(dve)
                dve.wait(tick, t_g, t_base)
                tg = dve.do(lambda e, t=t, pr=pr: e.tensor_tensor(pr[:], bank[:, acc[t], :], gt[:, 0, :], ALU.mult), c_res)
                acc_free[t] = (tg,)
                dve.wait(tg)
                tres = dve.do(lambda e, t=t, pr=pr: e.tensor_tensor(x_rows[:, t, :], pr[:], x_rows[:, t, :], ALU.add), c_res)
                gated.free(pi, tres)
            sp.wait(tres)
            rows_free = (load("x_out", out[b].rearrange("(t p) d -> p t d", p=P), x_rows[:]),)
        block()


_INS = ["x", "ctx_1024", "cond_1024"] + ["L0_xcond_" + n for n in (
    "Wq", "bq", "Wkv", "bkv", "Wp", "bp", "Wss_q", "bss_q", "Wss_kv", "bss_kv")] + ["L1_xcond_" + n for n in (
    "W_mod", "b_mod", "W_qkv", "b_qkv", "W_proj", "b_proj", "W_qc", "b_qc", "W_kvc", "b_kvc", "W_cproj", "b_cproj",
    "W_mlp1", "b_mlp1", "W_mlp2", "b_mlp2")]


def kernel(**inputs):
    import numpy as _np
    import concourse.bacc as _bacc
    from concourse import mybir as _mybir
    from concourse.bass_utils import run_bass_kernel_spmd as _run

    nc = _bacc.Bacc("TRN2", target_bir_lowering=False, num_devices=1)
    arrays, args = {}, {}
    for name in _INS:
        v = _np.ascontiguousarray(inputs[name])
        arrays[f"in_{name}"] = v
        args[name] = nc.dram_tensor(f"in_{name}", v.shape, _mybir.dt.from_np(v.dtype), kind="ExternalInput").ap()
    out = nc.dram_tensor("out", (B, N, D), F32, kind="ExternalOutput").ap()
    build(nc, args, out)
    r = _run(nc, [arrays], core_ids=[0])
    return r.results[0]["out"]
```

```python
from contextlib import ExitStack

from concourse import mybir

F32 = mybir.dt.float32
F32R = mybir.dt.float32r
ALU = mybir.AluOpType
ACT = mybir.ActivationFunctionType
AX_X = mybir.AxisListType.X

P = 128
B, N, D = 8, 512, 512
S = 77
NH, HD = 16, 32
GH = P // HD
G = NH // GH
KC = D // P
NT = N // P
HID = 4 * D
SCALE = float(HD) ** -0.5
ST = 3 * HD
ST_MAX = ST + 2
SP_ = S + 1


class Tick:

    def __init__(self, sem, value):
        self.sem, self.value = sem, value


class Count:

    def __init__(self, sem):
        self.sem, self.value = sem, 0

    def next(self, by):
        self.value += by
        return Tick(self.sem, self.value)


class Lane:

    def __init__(self):
        self.queue, self.waited = [], {}

    def wait(self, *ticks):
        for t in ticks:
            if t is not None and self.waited.get(id(t.sem), 0) < t.value:
                self.waited[id(t.sem)] = t.value
                self.queue.append(lambda e, t=t: e.wait_ge(t.sem, t.value))

    def do(self, make, signal=None, by=1):
        tick = signal.next(by) if signal is not None else None
        if tick is None:
            self.queue.append(make)
        else:
            self.queue.append(lambda e: make(e).then_inc(tick.sem, by))
        return tick

    def emit(self, engine):
        for make in self.queue:
            make(engine)
        self.queue = []


class Ring:

    def __init__(self, slots):
        self.slots, self.freed = list(slots), [()] * len(slots)
        self.idle = list(range(len(slots)))

    def take(self, *writers):
        i = self.idle.pop(0)
        for lane in writers:
            lane.wait(*self.freed[i])
        return i, self.slots[i]

    def free(self, i, *ticks):
        self.freed[i] = ticks
        if i not in self.idle:
            self.idle.append(i)


def build(nc, a, out):
    with ExitStack() as program:
        _build(nc, a, out, program)


def _build(nc, a, out, program):
    def dram(name, shape):
        return nc.dram_tensor(name, shape, F32, kind="Internal").ap()

    x1, x2, x3 = (dram(f"x{i}", (B, N, D)) for i in (1, 2, 3))
    q_parts = {s: dram(f"q_parts_{s}", (B, G, 2, P, N)) for s in ("L0", "self", "cross")}
    k_self = dram("k_parts_self", (B, G, 2, P, N))
    v_self = dram("v_self", (B, N, D))
    k_ctx = [dram(f"k_parts_ctx{l}", (2, D, B * S)) for l in (0, 1)]
    v_ctx = [dram(f"v_ctx{l}", (B, S, D)) for l in (0, 1)]
    gate_rows = dram("gate_rows", (2, 2, B, D))

    pe, act, dve, pool, sp = (Lane() for _ in range(5))

    def count(name):
        return Count(program.enter_context(nc.semaphore(name)))

    c_const, c_vconst = count("pool_constants"), count("vector_constants")
    c_norm, c_rstd = count("vector_norm_steps"), count("pool_rstd_steps")
    c_turn = count("tensor_transposes")
    c_wide, c_hi, c_lo = count("scalar_float32_values"), count("scalar_hi_parts"), count("vector_lo_parts")
    c_proj, c_res = count("tensor_projections"), count("vector_residuals")
    c_smax, c_negmax = count("tensor_scores_for_max"), count("vector_negated_maxima")
    c_score, c_exp = count("tensor_scores_by_key"), count("scalar_exponentials")
    c_av, c_out = count("tensor_value_sums"), count("vector_normalised_heads")
    c_xb, c_pair = count("pool_residual_bases"), count("pool_exponential_pairs")
    c_sum = count("pool_residuals")
    c_wlo = count("vector_weight_lo_parts")
    dma_counts = {}

    def dma_count(name):
        if name not in dma_counts:
            dma_counts[name] = count(f"dma_{name}")
        return dma_counts[name]

    def load(name, dst, src, lane=sp):
        return lane.do(lambda e: e.dma_start(dst, src), dma_count(name), 16)

    def raw(ap):
        return ap.bitcast(F32)

    stage_name = ["program"]

    def store_parts(name, dst, tile):
        return load(name, dst.rearrange("s f t -> f s t"), raw(tile[:]))

    def fetch_stack(name, stack, src, order):
        for r, s in enumerate(order):
            t = load(name, raw(stack[r * HD:(r + 1) * HD, :, :]), src[s].rearrange("(h p) t -> p h t", p=HD))
        return t

    bank = program.enter_context(nc.psum_tensor("banks", [P, 8, 512], F32))

    def sb(ctx, name, shape, dt=F32):
        return ctx.enter_context(nc.sbuf_tensor(f"{stage_name[0]}_{name}", shape, dt))

    ident = sb(program, "identity", [P, P])
    ones = sb(program, "ones", [P, HD])
    minus_half = sb(program, "minus_half", [P, NT])
    weight_stage = Ring([sb(program, f"weight_stage{i}", [P, 512]) for i in range(4)])
    norm_stats, norm_mean_var = sb(program, "norm_stats", [P, NT, 6]), sb(program, "norm_mean_var", [P, NT, 2])
    norm_rstd, norm_x = sb(program, "norm_rstd", [P, NT]), sb(program, "norm_x", [P, NT, D])
    MODS = ["L0q_scale", "L0q_shift", "L0kv_scale", "L0kv_shift", "a_shift", "a_scale", "m_shift", "m_scale"]
    mod_col = sb(program, "modulation_columns", [P, len(MODS), KC, B])
    BIAS_COLS = [("L0_bq", D), ("L0_bkv", D), ("L1_b_qkv", 2 * D), ("L1_b_qc", D), ("L1_b_kvc", D), ("L1_b_mlp1", HID),
                 ("L0_bss_q", 2 * D), ("L0_bss_kv", 2 * D), ("L1_b_mod", 6 * D), ("L1_b_proj", D), ("L1_b_mlp2", D)]
    bias_col = {}
    n_bias = sum(n for _, n in BIAS_COLS) // P
    bias_cols = sb(program, "bias_columns", [P, n_bias])

    def block():
        with nc.Block() as blk:
            @blk.tensor
            def _(e):
                pe.emit(e)

            @blk.scalar
            def _(e):
                act.emit(e)

            @blk.vector
            def _(e):
                dve.emit(e)

            @blk.gpsimd
            def _(e):
                pool.emit(e)

            @blk.sync
            def _(e):
                for c in dma_counts.values():
                    sp.wait(Tick(c.sem, c.value))
                sp.emit(e)


    class Weights:

        def __init__(self, ctx, name, w):
            self.hi, self.lo = (sb(ctx, f"{name}_{p}", [P, w.shape[0] // P, w.shape[1]], F32R) for p in ("hi", "lo"))
            self.ready = {}

    def columns_of(w, m):
        return w, m, (0, w.shape[0] // P), (m * P, (m + 1) * P)

    def chunk_of(w, c):
        return w, c, (c, c + 1), (0, w.shape[1])

    class Stream:

        def __init__(self, pieces, ahead=3):
            self.pieces, self.ahead, self.loaded, self.done = pieces, ahead, [], 0

        def run_ahead(self):
            while len(self.loaded) < len(self.pieces) and len(self.loaded) - self.done < self.ahead:
                w, _, (c0, c1), (n0, n1) = self.pieces[len(self.loaded)]
                i, buf = weight_stage.take(sp)
                view = buf[:].rearrange("p (c n) -> p c n", n=n1 - n0)
                self.loaded.append((i, view, load(f"stage{i}", view, w[c0 * P:c1 * P, n0:n1].rearrange(
                    "(c p) n -> p c n", p=P))))

        def split(self, weights):
            self.run_ahead()
            i, view, t = self.loaded[self.done]
            _, key, chunks, cols = self.pieces[self.done]
            self.done += 1
            hi, lo = (part[:, chunks[0]:chunks[1], cols[0]:cols[1]] for part in (weights.hi, weights.lo))
            act.wait(t)
            th = act.do(lambda e: e.copy(hi, view), c_hi)
            dve.wait(t, th)
            tl = dve.do(lambda e: e.tensor_tensor(lo, view, raw(hi), ALU.subtract), c_wlo)
            weight_stage.free(i, th, tl)
            weights.ready[key] = (th, tl)
            self.run_ahead()

    def weave(*generators):
        left = [g for g in generators if g is not None]
        while left:
            for g in list(left):
                if next(g, StopIteration) is StopIteration:
                    left.remove(g)

    def after(steps, generator):
        for _ in range(steps):
            yield
        yield from generator

    def parts_of(src, wide, hi, lo, produced, bias=None, scale=1.0):
        act.wait(*produced)
        kw = {} if bias is None and scale == 1.0 else {"bias": 0.0 if bias is None else bias, "scale": scale}
        fn = ACT.Copy if not kw else ACT.Identity
        wi, w = wide.take(act)
        tw = act.do(lambda e: e.activation(w[:, 0:src.shape[1]], src, fn, **kw), c_wide)
        th = act.do(lambda e: e.activation(hi, src, fn, **kw), c_hi)
        dve.wait(th)
        tl = dve.do(lambda e: e.tensor_tensor(lo, w[:, 0:src.shape[1]], raw(hi), ALU.subtract), c_lo)
        wide.free(wi, tl)
        return th, tl

    norm_x_free = [()]

    class Norm:

        def __init__(self, eps, mods, source):
            self.eps, self.mods, self.source = eps, mods, source

        def into(self, wide, psum, parts):
            self.wide, self.psum, self.parts = wide, psum, parts

        def batch(self, b, st):
            xn, stats, mean_var, rstd = norm_x, norm_stats, norm_mean_var, norm_rstd
            sp.wait(*norm_x_free[0])
            t_x = load("x_norm", xn[:], self.source[b].rearrange("(t p) d -> p t d", p=P))
            yield
            dve.wait(t_x)
            for t in range(NT):
                s = dve.do(lambda e, t=t: e.bn_stats(stats[:, t, :], xn[:, t, :]), c_norm)
                yield
            dve.wait(s)
            for t in range(NT):
                s = dve.do(lambda e, t=t: e.bn_aggr(mean_var[:, t, :], stats[:, t, :]), c_norm)
            pool.wait(s)
            s2 = pool.do(lambda e: e.tensor_scalar(rstd[:], mean_var[:, :, 1], self.eps, None, ALU.add), c_rstd)
            pool.wait(s2)
            s2 = pool.do(lambda e: e.tensor_tensor(rstd[:], rstd[:], minus_half[:], ALU.pow), c_rstd)
            yield
            dve.wait(s, s2)
            for t in range(NT):
                ready = dve.do(lambda e, t=t: e.tensor_scalar(
                    xn[:, t, :], xn[:, t, :], mean_var[:, t, 0:1], rstd[:, t:t + 1], ALU.subtract, ALU.mult), c_norm)
                yield
            st["parts_i"], (xh, xl) = self.parts.take(act, dve)
            st["xh"], st["xl"], st["t_parts"] = xh, xl, []
            for c in range(KC):
                i, bk = self.psum.take(pe)
                pe.wait(ready)
                for t in range(NT):
                    tp = pe.do(lambda e, c=c, t=t, bk=bk: e.transpose(
                        bank[:, bk, t * P:(t + 1) * P], xn[:, t, c * P:(c + 1) * P], ident[:, :]),
                        c_turn if t == NT - 1 else None)
                kw = {}
                if self.mods:
                    sc, sh = (MODS.index(m) for m in self.mods)
                    kw = {"scale": mod_col[:, sc, c, b:b + 1], "bias": mod_col[:, sh, c, b:b + 1]}
                th, tl = parts_of(bank[:, bk, :], self.wide, xh[:, c, :], xl[:, c, :], (tp,), **kw)
                self.psum.free(i, th)
                st["t_parts"] += [th, tl]
                if c == KC - 1:
                    norm_x_free[0] = (tp,)
                yield

    class Start:
        STEPS = 1 + NT + 1 + NT

        def __init__(self, norm, stream):
            self.norm, self.stream, self.batch0 = norm, stream, {}

        def begin(self):
            sp.wait(first_stored[0])
            self.turning = self.norm.batch(0, self.batch0)
            next(self.turning)
            self.stream.run_ahead()
            yield
            for k in range(self.STEPS - 1):
                if k != NT + 1:
                    next(self.turning)
                yield
            next(self.turning)

    first_stored = [None]

    def product_steps(out_ap, pairs, done, at_once=3):
        terms = [(l, r) for lh, ll, rh, rl in pairs for l, r in ((lh, rh), (lh, rl), (ll, rh))]
        for k, (l, r) in enumerate(terms):
            last = k == len(terms) - 1
            tick = pe.do(lambda e, l=l, r=r, k=k, last=last: e.matmul(out_ap, l, r, start=k == 0, stop=last),
                         c_proj if last else None)
            if last:
                done.append(tick)
            elif k % at_once == at_once - 1:
                yield

    def product(out_ap, pairs):
        done = []
        weave(product_steps(out_ap, pairs, done))
        return done[0]

    w_up, w_down = a["L1_xcond_W_mlp1"], a["L1_xcond_W_mlp2"]
    JC = HID // P
    UP_AHEAD = 3
    starts = {
        "L0": Start(Norm(1e-5, ("L0q_scale", "L0q_shift"), a["x"]),
                    Stream([columns_of(a["L0_xcond_Wq"], m) for m in range(G)]
                           + [chunk_of(a["L0_xcond_Wp"], c) for c in range(KC)])),
        "qkv": Start(Norm(1e-6, ("a_scale", "a_shift"), x1),
                     Stream([columns_of(a["L1_xcond_W_qkv"], m) for m in range(3 * G)])),
        "cross": Start(Norm(1e-6, None, x2),
                       Stream([columns_of(a["L1_xcond_W_qc"], m) for m in range(G)]
                              + [chunk_of(a["L1_xcond_W_cproj"], c) for c in range(KC)])),
        "mlp": Start(Norm(1e-6, ("m_scale", "m_shift"), x3),
                     Stream([columns_of(w_up, m) for m in range(UP_AHEAD)]
                            + [piece for j in range(JC) for piece in
                               [chunk_of(w_down, j)] + ([columns_of(w_up, j + UP_AHEAD)] if j + UP_AHEAD < JC else [])]))}

    with ExitStack() as ctx:
        stage_name[0] = "prepare"
        CT = B * S
        HALF = CT // 2
        TT = -(-CT // P)
        rows_of = lambda t: min(P, CT - t * P)
        cond = sb(ctx, "cond_rows", [B, D])
        silu = sb(ctx, "silu_rows", [B, D])
        cond_T = sb(ctx, "silu_cond_columns", [P, KC, HD])
        wbuf = Ring([sb(ctx, f"mod_weights{i}", [P, KC, D]) for i in range(2)])
        mod_rows = Ring([sb(ctx, f"modulation_rows{i}", [P, P]) for i in range(2)])
        gate_cols = sb(ctx, "gate_columns", [P, 2, 2, KC, B])
        gate_turned = sb(ctx, "gates_turned", [P, P])
        bias_chunks = sb(ctx, "bias_chunks", [n_bias, P])
        xc = sb(ctx, "context_rows", [P, TT, D])
        stats, mean_var = sb(ctx, "stats", [P, TT, 6]), sb(ctx, "mean_var", [P, TT, 2])
        rstd = sb(ctx, "rstd", [P, TT])
        xn = sb(ctx, "context_normed", [P, TT, D])
        xT = sb(ctx, "context_turned", [P, KC, CT])
        parts = [[sb(ctx, f"context_{p}{l}", [P, KC, CT], F32R) for p in ("hi", "lo")] for l in (0, 1)]
        wide = Ring([sb(ctx, f"wide{i}", [P, 512]) for i in range(2)])
        kst = Ring([sb(ctx, f"key_parts{i}", [P, 2, HALF], F32R) for i in range(3)])
        vst = Ring([sb(ctx, f"value_rows{i}", [P, D]) for i in range(2)])
        bv = [sb(ctx, f"value_bias{l}", [P, D]) for l in (0, 1)]
        psum = Ring(range(8))
        w_kv = [a["L0_xcond_Wkv"], a["L1_xcond_W_kvc"]]
        weights = [Weights(ctx, f"w_kv{l}", w) for l, w in enumerate(w_kv)]
        stream = Stream([columns_of(w_kv[l], m) for l in (1, 0) for m in range(2 * G)], 1)
        key_bias = ["L0_bkv", "L1_b_kvc"]
        EPS = [1e-5, 1e-6]

        t = pool.do(lambda e: e.memset(ident[:], 0.0), c_const)
        pool.do(lambda e: e.memset(ones[:], 1.0), c_const)
        pool.do(lambda e: e.memset(minus_half[:], -0.5), c_const)
        pool.wait(t)
        t_ident = pool.do(lambda e: e.affine_select(
            out=ident[:], in_=ident[:], compare_op=ALU.not_equal, fill=1.0, base=0,
            pattern=[[-1, P]], channel_multiplier=1), c_const)

        flat = a["ctx_1024"].rearrange("b s d -> (b s) d")
        full = CT // P
        t_cond = load("cond", cond[:], a["cond_1024"])
        load("ctx", xc[:, 0:full, :], flat[0:full * P].rearrange("(t p) d -> p t d", p=P))
        t_x = load("ctx", xc[0:CT - full * P, full, :], flat[full * P:CT])
        at = 0
        for bname, n in BIAS_COLS:
            bias_col[bname] = at
            t_cols = load("bias_chunks", bias_chunks[at:at + n // P, :],
                          a[bname.replace("_", "_xcond_", 1)][0:n].rearrange("(c p) -> c p", p=P))
            at += n // P
        for l, bname in enumerate(("L0_xcond_bkv", "L1_xcond_b_kvc")):
            t_bv = load("value_bias", bv[l][:], a[bname][D:2 * D].partition_broadcast(P))

        def modulation():
            act.wait(t_cond)
            t = act.do(lambda e: e.activation(silu[:], cond[:], ACT.Exp, scale=-1.0), c_exp)
            dve.wait(t)
            t = dve.do(lambda e: e.tensor_scalar(silu[:], silu[:], 1.0, None, ALU.add), c_norm)
            dve.wait(t)
            t = dve.do(lambda e: e.reciprocal(silu[:], silu[:]), c_norm)
            dve.wait(t)
            t_silu = dve.do(lambda e: e.tensor_tensor(silu[:], cond[:], silu[:], ALU.mult), c_norm)
            t_zero = dve.do(lambda e: e.memset(cond_T[:], 0.0), c_vconst)
            pi, bk = psum.take(pe)
            pe.wait(t_silu, t_ident)
            for c in range(KC):
                t = pe.do(lambda e, c=c, bk=bk: e.transpose(bank[:, bk, c * B:(c + 1) * B], silu[:, c * P:(c + 1) * P],
                                                            ident[0:B, 0:B]), c_turn)
            dve.wait(t, t_zero)
            t_condT = dve.do(lambda e, bk=bk: e.tensor_copy(
                cond_T[:, :, 0:B], bank[:, bk, 0:KC * B].rearrange("p (c b) -> p c b", b=B)), c_norm)
            psum.free(pi, t_condT)
            pi, bk = psum.take(pe)
            pe.wait(t_cols)
            t = pe.do(lambda e, bk=bk: e.transpose(bank[:, bk, 0:n_bias], bias_chunks[:], ident[0:n_bias, 0:n_bias]), c_turn)
            act.wait(t)
            t_bias = act.do(lambda e, bk=bk: e.copy(bias_cols[:], bank[:, bk, 0:n_bias]), c_wide)
            psum.free(pi, t_bias)
            sources = [(f"L0{x}_{what}", f"L0_xcond_Wss_{x}", f"L0_bss_{x}", part)
                       for x in ("kv", "q") for part, what in enumerate(("scale", "shift"))]
            sources += [(n, "L1_xcond_W_mod", "L1_b_mod", part) for part, n in enumerate(
                ("a_shift", "a_scale", "a_gate", "m_shift", "m_scale", "m_gate"))]
            for dst_name, wname, bname, part in sources:
                i, w = wbuf.take(sp)
                t_w = load(f"mod_w{i}", w[:], a[wname][:, part * D:(part + 1) * D].rearrange("(c p) n -> p c n", p=P))
                yield
                pi, bk = psum.take(pe)
                pe.wait(t_w, t_condT)
                for c in range(KC):
                    for k in range(KC):
                        t = pe.do(lambda e, c=c, k=k, w=w, bk=bk: e.matmul(
                            bank[k * HD:(k + 1) * HD, bk, 0:P], cond_T[:, c, :], w[:, c, k * P:(k + 1) * P],
                            start=c == 0, stop=c == KC - 1), c_proj)
                wbuf.free(i, t)
                ri, row = mod_rows.take(act)
                act.wait(t)
                t = act.do(lambda e, bk=bk, row=row: e.copy(row[:], bank[:, bk, 0:P]), c_wide)
                psum.free(pi, t)
                yield
                pi, bk = psum.take(pe)
                pe.wait(t)
                t = pe.do(lambda e, bk=bk, row=row: e.transpose(bank[:, bk, 0:P], row[:], ident[:]), c_turn)
                mod_rows.free(ri, t)
                dve.wait(t, t_bias)
                gate = {"a_gate": 0, "m_gate": 1}.get(dst_name)
                dst = mod_col[:, MODS.index(dst_name), :, :] if gate is None else gate_cols[:, gate, 0, :, :]
                col = bias_col[bname] + part * KC
                one = 1.0 if dst_name.endswith("scale") else 0.0
                t = dve.do(lambda e, bk=bk, dst=dst, col=col, one=one: e.scalar_tensor_tensor(
                    dst, bank[:, bk, 0:P].rearrange("p (c b) -> p c b", b=HD)[:, :, 0:B], one,
                    bias_cols[:, col:col + KC].unsqueeze(2).broadcast_to([P, KC, B]), ALU.add, ALU.add), c_norm)
                psum.free(pi, t)
                made[dst_name] = t
                if gate is not None:
                    dve.wait(t)
                    col = bias_col["L1_b_mlp2" if gate else "L1_b_proj"]
                    t = dve.do(lambda e, gate=gate, col=col: e.tensor_tensor(
                        gate_cols[:, gate, 1, :, :], gate_cols[:, gate, 0, :, :],
                        bias_cols[:, col:col + KC].unsqueeze(2).broadcast_to([P, KC, B]), ALU.mult), c_norm)
                yield
            pi, bk = psum.take(pe)
            pe.wait(t)
            t = pe.do(lambda e, bk=bk: e.transpose(
                bank[:, bk, 0:P], gate_cols[:].rearrange("p g w c b -> p (g w c b)"), ident[:]), c_turn)
            act.wait(t)
            t = act.do(lambda e, bk=bk: e.copy(gate_turned[:], bank[:, bk, 0:P]), c_wide)
            psum.free(pi, t)
            pool.wait(t)
            for k in range(4):
                load("gates_out", gate_rows[k // 2, k % 2].rearrange("b (c n) -> c b n", n=P),
                     gate_turned[k * KC * B:(k + 1) * KC * B, :], pool)

        made = {}

        def statistics():
            dve.wait(t_x)
            for t in range(TT):
                r = rows_of(t)
                s = dve.do(lambda e, t=t, r=r: e.bn_stats(stats[0:r, t, :], xc[0:r, t, :]), c_norm)
            dve.wait(s)
            for t in range(TT):
                r = rows_of(t)
                s = dve.do(lambda e, t=t, r=r: e.bn_aggr(mean_var[0:r, t, :], stats[0:r, t, :]), c_norm)
            return s

        free = {"xn": (), "rstd": (), "xT": ()}

        def context_parts(l, aggregated):
            xh, xl = parts[l]
            pool.wait(aggregated, *free["rstd"])
            for r, t0, t1 in ((P, 0, full), (CT - full * P, full, TT)):
                s = pool.do(lambda e, r=r, t0=t0, t1=t1: e.tensor_scalar(
                    rstd[0:r, t0:t1], mean_var[0:r, t0:t1, 1], EPS[l], None, ALU.add), c_rstd)
                pool.wait(s)
                s = pool.do(lambda e, r=r, t0=t0, t1=t1: e.tensor_tensor(
                    rstd[0:r, t0:t1], rstd[0:r, t0:t1], minus_half[0:r, 0:t1 - t0], ALU.pow), c_rstd)
            yield
            dve.wait(s, aggregated, *free["xn"])
            for t in range(TT):
                r = rows_of(t)
                normed = dve.do(lambda e, t=t, r=r: e.tensor_scalar(
                    xn[0:r, t, :], xc[0:r, t, :], mean_var[0:r, t, 0:1], rstd[0:r, t:t + 1],
                    ALU.subtract, ALU.mult), c_norm)
                yield
            free["rstd"] = (normed,)
            pe.wait(normed, t_ident)
            for c in range(KC):
                for t0, t1 in ((0, full), (full, TT)):
                    bi, bk = psum.take(pe)
                    w_ = sum(rows_of(t) for t in range(t0, t1))
                    for t in range(t0, t1):
                        r = rows_of(t)
                        tp = pe.do(lambda e, c=c, t=t, r=r, bk=bk, t0=t0: e.transpose(
                            bank[:, bk, (t - t0) * P:(t - t0) * P + r], xn[0:r, t, c * P:(c + 1) * P],
                            ident[0:r, 0:r]), c_turn)
                    act.wait(tp, *free["xT"])
                    tw = act.do(lambda e, c=c, t0=t0, w_=w_, bk=bk: e.activation(
                        xT[:, c, t0 * P:t0 * P + w_], bank[:, bk, 0:w_], ACT.Copy), c_wide)
                    psum.free(bi, tw)
                if l == 0:
                    act.wait(tw, made["L0kv_scale"], made["L0kv_shift"])
                    for b in range(B):
                        tw = act.do(lambda e, c=c, b=b: e.activation(
                            xT[:, c, b * S:(b + 1) * S], xT[:, c, b * S:(b + 1) * S], ACT.Identity,
                            bias=mod_col[:, 3, c, b:b + 1], scale=mod_col[:, 2, c, b:b + 1]), c_wide)
                act.wait(tw)
                th = act.do(lambda e, c=c: e.copy(xh[:, c, :], xT[:, c, :]), c_hi)
                dve.wait(th)
                tl = dve.do(lambda e, c=c: e.tensor_tensor(xl[:, c, :], xT[:, c, :], raw(xh[:, c, :]), ALU.subtract), c_lo)
                ready[l].extend((th, tl))
                yield
            free["xn"], free["xT"] = (tp,), (tl,)

        ready = ([], [])

        def weight_columns(l):
            for m in range(2 * G):
                stream.split(weights[l])
                yield

        def context_products(l, lane):
            xh, xl = parts[l]
            wh, wl = weights[l].hi, weights[l].lo
            bcol = bias_col[key_bias[l]]
            pe.wait(*ready[l])
            for g in range(G):
                pe.wait(*weights[l].ready[g])
                for h in range(2):
                    bi, bk = psum.take(pe)
                    cols = slice(h * HALF, (h + 1) * HALF)
                    f = slice(g * P, (g + 1) * P)
                    tp = product(bank[:, bk, 0:HALF], [(wh[:, c, f], wl[:, c, f], xh[:, c, cols], xl[:, c, cols])
                                                      for c in range(KC)])
                    ki, kt = kst.take(act, dve)
                    th, tl = parts_of(bank[:, bk, 0:HALF], wide, kt[:, 0, :], kt[:, 1, :], (tp,),
                                      bias=bias_cols[:, bcol + g:bcol + g + 1])
                    psum.free(bi, th)
                    lane.wait(th, tl)
                    t = load(f"context{l}_key_store{ki}", k_ctx[l][:, f, cols].rearrange("s p t -> p s t"), raw(kt[:]), lane)
                    kst.free(ki, t)
                    yield
            pe.wait(*(t for g in range(G) for t in weights[l].ready[G + g]))
            values_flat = v_ctx[l].rearrange("b s d -> (b s) d")
            for t in range(TT):
                bi, bk = psum.take(pe)
                r = slice(t * P, t * P + rows_of(t))
                rows = rows_of(t)
                tp = product(bank[0:rows, bk, :], [(xh[:, c, r], xl[:, c, r], wh[:, c, D:2 * D], wl[:, c, D:2 * D])
                                                  for c in range(KC)])
                vi, vt = vst.take(dve)
                dve.wait(tp, t_bv)
                tv = dve.do(lambda e, bk=bk, vt=vt, rows=rows: e.tensor_tensor(
                    vt[0:rows, :], bank[0:rows, bk, :], bv[l][0:rows, :], ALU.add), c_res)
                psum.free(bi, tv)
                lane.wait(tv)
                vst.free(vi, load(f"context{l}_value_store{vi}", values_flat[r, :], vt[0:rows, :], lane))
                yield

        modulating = modulation()
        next(modulating)
        aggregated = statistics()
        first = (next(modulating) for _ in range(10))
        weave(first, context_parts(1, aggregated), weight_columns(1), first)
        turned = context_parts(0, aggregated)
        next(turned)
        weave(weight_columns(0), context_products(1, pool), turned, modulating)
        weave(context_products(0, sp), modulating, starts["L0"].begin())
        block()

    def attention_stage(name, x_in, x_out, bq, wp, bp, layer, following):
        own_q = layer is not None
        keys = S if own_q else P
        KT = 1 if own_q else NT
        with ExitStack() as ctx:
            stage_name[0] = name
            x_ring = Ring([sb(ctx, "x_rows", [P, NT, D])])
            QUERY, FETCH, MAX, ROWS = (5, 4, 3, 2) if own_q else (4, 3, 2, 1)
            q_ring = Ring([sb(ctx, f"query_stack{i}", [ST_MAX, GH, N], F32R) for i in range(FETCH + 1)])
            if own_q:
                k_ring = Ring([sb(ctx, f"key_stack{i}", [ST_MAX, NH, SP_], F32R) for i in range(2)])
            else:
                k_ring = Ring([sb(ctx, f"key_stack{i}", [ST_MAX, GH, N], F32R) for i in range(4)])
            v_ring = Ring([sb(ctx, f"values{i}", [keys, KT, D]) for i in range(2)])
            p_ring = Ring([sb(ctx, f"exponentials{i}", [keys, GH, N]) for i in range(2 if own_q else 4)])
            o_ring = Ring([(sb(ctx, f"heads_hi{i}", [P, G, N], F32R), sb(ctx, f"heads_lo{i}", [P, G, N], F32R))
                           for i in range(2)])
            sums_turned = sb(ctx, "sums_turned", [P, N])
            recip_turned = sb(ctx, "reciprocals_turned", [P, N // HD])
            recip = sb(ctx, "reciprocal_sums", [P, N])
            o_wide = Ring([sb(ctx, f"heads_float32_{i}", [P, N]) for i in range(2)])
            negmax = Ring([sb(ctx, f"negated_max{i}", [P, GH * NT]) for i in range(2)])
            max_rows = Ring([sb(ctx, f"max_row_parts{i}", [GH * NT, 2, P], F32R) for i in range(2)])
            for i, k in enumerate(k_ring.slots):
                if own_q:
                    dve.do(lambda e, k=k: e.memset(raw(k[0:ST, :, S:SP_]), 0.0), c_vconst)
                t_ones = dve.do(lambda e, k=k: e.memset(raw(k[ST:ST_MAX]), 1.0), c_vconst)
                k_ring.free(i, t_ones)
            work, heads, sums = Ring(range(6)), Ring([6]), Ring([7])
            if own_q:
                wide = Ring([sb(ctx, f"wide{i}", [P, N]) for i in range(2)])
                parts = Ring([(sb(ctx, "x_hi", [P, KC, N], F32R), sb(ctx, "x_lo", [P, KC, N], F32R))])
                start = starts[name]
                norm = start.norm
                norm.into(wide, work, parts)
                q_out = Ring([sb(ctx, f"query_parts{i}", [P, 2, N], F32R) for i in range(2)])
                stream = start.stream
                w_q = Weights(ctx, "w_q", stream.pieces[0][0])
                bias_tile = sb(ctx, "projection_bias", [P, D])
                t_bias = load("projection_bias", bias_tile[:], bp.partition_broadcast(P))
            else:
                gate = Ring([sb(ctx, f"gate_and_bias{i}", [P, 2, D]) for i in range(2)])
                stream = Stream([chunk_of(wp, c) for c in range(KC)])
                gated_rows = Ring([sb(ctx, "gated_rows", [P, D])])
            w_p = Weights(ctx, "w_proj", wp)
            batch = [start.batch0 if own_q and b == 0 else {} for b in range(B)]
            group = {(b, g): {} for b in range(B) for g in range(G)}

            def load_keys(b):
                if own_q:
                    st = batch[b]
                    st["ki"], st["k"] = k_ring.take(sp)
                    src = k_ctx[layer][:, :, b * S:(b + 1) * S].rearrange("s (h p) t -> s p h t", p=HD)
                    for r, s in ((0, 0), (1, 0), (2, 1)):
                        st["t_k"] = load(f"k{st['ki']}", raw(st["k"][r * HD:(r + 1) * HD, :, 0:S]), src[s])

            def load_values(b):
                st = batch[b]
                st["vi"], st["v"] = v_ring.take(sp)
                src = v_ctx[layer][b].unsqueeze(1) if own_q else v_self[b].rearrange("(t p) d -> p t d", p=P)
                st["t_v"] = load(f"v{st['vi']}", st["v"][:], src)

            def load_base(b):
                st = batch[b]
                st["xi"], st["x"] = x_ring.take(sp)
                st["t_x"] = load("x_rows", st["x"][:], x_in[b].rearrange("(t p) d -> p t d", p=P))
                if not own_q:
                    st["gi"], st["gate"] = gate.take(sp)
                    for w in range(2):
                        st["t_gate"] = load(f"gate{st['gi']}", st["gate"][:, w, :],
                                            gate_rows[0, w, b].partition_broadcast(P))

            def add_base(b):
                st = batch[b]
                rhs, t_rhs = (bias_tile[:], t_bias) if own_q else (st["gate"][:, 1, :], st["t_gate"])
                pool.wait(st["t_x"], t_rhs)
                st["t_base"] = [pool.do(lambda e, t=t: e.tensor_tensor(
                    st["x"][:, t, :], st["x"][:, t, :], rhs, ALU.add), c_xb) for t in range(NT)]

            def query(b, g):
                st = batch[b]
                xh, xl, hi, lo = st["xh"], st["xl"], w_q.hi, w_q.lo
                pi, bk = work.take(pe)
                pe.wait(*w_q.ready[g])
                pe.wait(*st["t_parts"])
                f = slice(g * P, (g + 1) * P)
                done = []
                yield from product_steps(bank[:, bk, :], [(hi[:, c, f], lo[:, c, f], xh[:, c, :], xl[:, c, :]) for c in range(KC)], done)
                tp = done[0]
                if g == G - 1:
                    parts.free(st["parts_i"], tp)
                qi, qt = q_out.take(act, dve)
                th, tl = parts_of(bank[:, bk, :], wide, qt[:, 0, :], qt[:, 1, :], (tp,),
                                  bias=bias_cols[:, bias_col[bq] + g:bias_col[bq] + g + 1])
                work.free(pi, th)
                sp.wait(th, tl)
                t = store_parts(f"q_store{qi}", q_parts[name][b, g], qt)
                q_out.free(qi, t)
                group[b, g]["stored"] = t
                yield

            def fetch(b, g):
                gr = group[b, g]
                sp.wait(gr.get("stored"))
                gr["qi"], gr["q"] = q_ring.take(sp)
                gr["t_q"] = fetch_stack(f"q{gr['qi']}", gr["q"], q_parts[name][b, g], (0, 1, 0))
                if not own_q:
                    gr["ki"], gr["k"] = k_ring.take(sp)
                    gr["t_k"] = fetch_stack(f"k{gr['ki']}", gr["k"], k_self[b, g], (0, 0, 1))

            def maxima(b, g):
                gr = group[b, g]
                if own_q:
                    gr["k"], gr["t_k"] = batch[b]["k"][:, g * GH:(g + 1) * GH, :], batch[b]["t_k"]
                ni, nm = negmax.take(dve)
                pe.wait(gr["t_q"], gr["t_k"])
                for qt in range(NT):
                    rows = slice(qt * P, (qt + 1) * P)
                    if own_q:
                        si, bk = work.take(pe)
                        for h in range(GH):
                            tp = pe.do(lambda e, h=h, bk=bk, rows=rows: e.matmul(
                                bank[:, bk, h * SP_:(h + 1) * SP_], gr["q"][0:ST, h, rows], gr["k"][0:ST, h, :],
                                start=True, stop=True), c_smax)
                        dve.wait(tp)
                        tn = dve.do(lambda e, bk=bk, qt=qt: e.tensor_reduce(
                            nm[:, qt:GH * NT:NT], bank[:, bk, 0:GH * SP_].rearrange("p (h k) -> p h k", k=SP_)[:, :, 0:S],
                            AX_X, ALU.max, negate=True), c_negmax)
                        work.free(si, tn)
                        yield
                    else:
                        for h in range(GH):
                            si, bk = work.take(pe)
                            tp = pe.do(lambda e, h=h, bk=bk, rows=rows: e.matmul(
                                bank[:, bk, :], gr["q"][0:ST, h, rows], gr["k"][0:ST, h, :],
                                start=True, stop=True), c_smax)
                            dve.wait(tp)
                            tn = dve.do(lambda e, bk=bk, qt=qt, h=h: e.tensor_reduce(
                                nm[:, h * NT + qt:h * NT + qt + 1], bank[:, bk, :], AX_X, ALU.max, negate=True), c_negmax)
                            work.free(si, tn)
                            yield
                gr["negmax"] = (ni, nm, tn)

            def max_rows_of(b, g):
                gr = group[b, g]
                ni, nm, tn = gr["negmax"]
                si, bk = work.take(pe)
                pe.wait(tn)
                tp = pe.do(lambda e: e.transpose(bank[0:GH * NT, bk, 0:P], nm[:], ident[:]), c_turn)
                negmax.free(ni, tp)
                mi, mr = max_rows.take(act, dve)
                act.wait(tp)
                th = act.do(lambda e: e.activation(mr[:, 0, :], bank[0:GH * NT, bk, 0:P], ACT.Copy), c_hi)
                dve.wait(th)
                tl = dve.do(lambda e: e.tensor_tensor(mr[:, 1, :], bank[0:GH * NT, bk, 0:P], raw(mr[:, 0, :]), ALU.subtract), c_lo)
                work.free(si, tl)
                sp.wait(th, tl, tp)
                for w in range(2):
                    gr["t_max"] = load(f"max{gr['qi']}", raw(gr["q"][ST + w:ST + w + 1].rearrange("a h (t q) -> a (h t) q", q=P)),
                                       raw(mr[:, w, :]))
                max_rows.free(mi, gr["t_max"])
                yield

            late = []

            def attend(b, g):
                gr, st = group[b, g], batch[b]
                pe.wait(gr["t_max"])
                for kt in range(KT):
                    pi, pt = p_ring.take(act)
                    cols = slice(kt * P, kt * P + keys)
                    for h in range(GH):
                        si, bk = work.take(pe)
                        tp = pe.do(lambda e, h=h, bk=bk, cols=cols: e.matmul(
                            bank[0:keys, bk, :], gr["k"][0:ST_MAX, h, cols], gr["q"][0:ST_MAX, h, :],
                            start=True, stop=True), c_score)
                        act.wait(tp)
                        te = act.do(lambda e, h=h, bk=bk, pt=pt: e.activation(
                            pt[:, h, :], bank[0:keys, bk, :], ACT.Exp, scale=SCALE), c_exp)
                        work.free(si, te)
                        yield
                        if h == (0 if own_q else 1):
                            while late:
                                values(*late.pop(0))
                    if kt == KT - 1:
                        q_ring.free(gr["qi"], tp)
                        if not own_q:
                            k_ring.free(gr["ki"], tp)
                        elif g == G - 1:
                            k_ring.free(st["ki"], tp)
                    late.append((b, g, kt, pi, pt, te))

            def heads_at_once(out_ap, weights, exps, start, stop):
                for h in range(GH):
                    t = pe.do(lambda e, h=h: e.matmul(out_ap[h * HD:(h + 1) * HD, :], weights(h), exps[:, h, :],
                                                      start=start, stop=stop), c_av)
                return t

            def values(b, g, kt, pi, pt, te):
                st, gr = batch[b], group[b, g]
                if kt % 2 == 1 and pair_sums:
                    sum_pair(*pair_sums.pop(0))
                if kt == 0:
                    gr["heads"] = heads.take(pe)[1]
                pe.wait(te, st["t_v"])
                tp = heads_at_once(bank[:, gr["heads"], :],
                                   lambda h: st["v"][:, kt, (g * GH + h) * HD:(g * GH + h + 1) * HD],
                                   pt, kt == 0, kt == KT - 1)
                if own_q:
                    sum_pair(b, g, kt, pi, pt, te)
                elif kt % 2 == 0:
                    gr["even"] = (pi, pt, tp)
                else:
                    even_pi, even_pt, even_tp = gr["even"]
                    pool.wait(te, even_tp)
                    t_add = pool.do(lambda e: e.tensor_tensor(even_pt[:], even_pt[:], pt[:], ALU.add), c_pair)
                    p_ring.free(pi, tp, t_add)
                    pair_sums.append((b, g, kt, even_pi, even_pt, t_add))
                if kt == KT - 1:
                    gr["t_heads"] = tp
                    if g == G - 1:
                        v_ring.free(st["vi"], tp)

            pair_sums = []

            def sum_pair(b, g, kt, pi, pt, ready):
                gr = group[b, g]
                first = kt <= 1
                if first:
                    gr["sums"] = sums.take(pe)[1]
                pe.wait(ready)
                tp = heads_at_once(bank[:, gr["sums"], :], lambda h: ones[0:keys, :], pt, first, kt == KT - 1)
                p_ring.free(pi, tp)
                if kt == KT - 1:
                    gr["t_sums"] = tp

            def finish(b, g):
                gr, st = group[b, g], batch[b]
                while "t_heads" not in gr:
                    yield
                if g == 0:
                    st["oi"], st["o"] = o_ring.take(act, dve)
                wi, w = o_wide.take(act)
                act.wait(gr["t_heads"])
                th = act.do(lambda e: e.copy(w[:], bank[:, gr["heads"], :]), c_wide)
                heads.free(0, th)
                while "t_sums" not in gr:
                    yield
                dve.wait(gr["t_sums"])
                t = dve.do(lambda e: e.transpose(sums_turned[:], bank[:, gr["sums"], :]), c_out)
                sums.free(0, t)
                yield
                dve.wait(t)
                t = dve.do(lambda e: e.reciprocal(recip_turned[:], sums_turned[:, 0:N:HD]), c_out)
                yield
                dve.wait(t)
                t = dve.do(lambda e: e.transpose(
                    recip[:].rearrange("p (a b) -> p a b", b=HD),
                    recip_turned[:].unsqueeze(2).broadcast_to([P, N // HD, HD])), c_out)
                yield
                dve.wait(t, th)
                to = dve.do(lambda e: e.tensor_tensor(w[:], w[:], recip[:], ALU.mult), c_out)
                oh, ol = st["o"]
                yield
                act.wait(to)
                th = act.do(lambda e: e.copy(oh[:, g, :], w[:]), c_hi)
                yield
                dve.wait(th)
                tl = dve.do(lambda e: e.tensor_tensor(ol[:, g, :], w[:], raw(oh[:, g, :]), ALU.subtract), c_lo)
                o_wide.free(wi, tl)
                st["t_o"] = (th, tl)

            def project(b):
                st = batch[b]
                oh, ol = st["o"]
                for t in range(NT):
                    pe.wait(*st["t_o"], *(x for c in range(KC) for x in w_p.ready[c]))
                    pi, bk = work.take(pe)
                    r = slice(t * P, (t + 1) * P)
                    done = []
                    yield from product_steps(bank[:, bk, :], [(oh[:, c, r], ol[:, c, r], w_p.hi[:, c, :], w_p.lo[:, c, :]) for c in range(KC)], done)
                    tp = done[0]
                    dve.wait(tp, st["t_base"][t])
                    if own_q:
                        tres = dve.do(lambda e, t=t, bk=bk: e.tensor_tensor(
                            st["x"][:, t, :], bank[:, bk, :], st["x"][:, t, :], ALU.add), c_res)
                        work.free(pi, tres)
                    else:
                        dve.wait(st["t_gate"])
                        wi, w = gated_rows.take(dve)
                        tg = dve.do(lambda e, bk=bk, w=w: e.tensor_tensor(w[:], bank[:, bk, :], st["gate"][:, 0, :], ALU.mult), c_res)
                        work.free(pi, tg)
                        pool.wait(tg)
                        tres = pool.do(lambda e, t=t, w=w: e.tensor_tensor(
                            st["x"][:, t, :], w[:], st["x"][:, t, :], ALU.add), c_sum)
                        gated_rows.free(wi, tres)
                    if t == NT - 1:
                        o_ring.free(st["oi"], tp)
                        if not own_q:
                            gate.free(st["gi"], tres)
                        sp.wait(tres)
                        stored = load("x_out", x_out[b].rearrange("(t p) d -> p t d", p=P), st["x"][:])
                        x_ring.free(st["xi"], stored)
                        if b == 0:
                            first_stored[0] = stored
                    yield

            seq = [(b, g) for b in range(B) for g in range(G)]
            last = len(seq)

            def of_group(make, n):
                return make(*seq[n]) if n < last else iter(())

            def norm_quarter(n):
                b, g = seq[n][0] + 1, seq[n][1]
                if b == B:
                    return None
                if g == 0:
                    batch[b]["turning"] = norm.batch(b, batch[b])
                    next(batch[b]["turning"])
                turning = batch[b]["turning"]
                if g == 1:
                    return (next(turning) for _ in range(NT + 1))
                if g == 2:
                    return after(1, (next(turning) for _ in range(NT)))
                return after(2, turning) if g == 3 else None

            if own_q:
                stream.split(w_q)
                load_keys(0)
                weave(start.turning, after(2, (stream.split(w_q) for _ in range(G - 1))))
                for n in range(G):
                    weave(query(*seq[n]), maxima(*seq[0]) if n == 3 else None,
                          norm_quarter(max(n - 1, 0)) if n != 1 else None)
                    fetch(*seq[n])
                load_values(0)
                weave(maxima(*seq[1]), max_rows_of(*seq[0]), norm_quarter(3))
                weave(query(*seq[4]), maxima(*seq[2]), max_rows_of(*seq[1]), norm_quarter(4))
            else:
                for n in range(FETCH):
                    fetch(*seq[n])
                load_values(0)
                for n in range(MAX):
                    weave(maxima(*seq[n]), max_rows_of(*seq[n - 1]) if n and n - 1 < ROWS else None)
            for n, (b, g) in enumerate(seq):
                if n < G:
                    stream.split(w_p)
                if g == 0 and b + 1 < B:
                    load_keys(b + 1)
                if n + FETCH < last:
                    fetch(*seq[n + FETCH])
                side = []
                if g == 1 and b > 0:
                    add_base(b - 1)
                    projecting = project(b - 1)
                if g > 0 and b > 0:
                    tiles = (0, 1, 2, 1)[g]
                    part = after(4 if g == 1 else 0, (next(projecting) for _ in range(tiles * KC)))
                    side += [part] * tiles
                asking = of_group(query, n + QUERY) if own_q else None
                quarter = (g + QUERY) % G
                if own_q and quarter == 0:
                    asking = after(2, asking)
                if n == last - G:
                    beginning = starts[following].begin()
                if n >= last - G:
                    side.append(next(beginning, None) for _ in range(Start.STEPS // G + 1))
                weave(attend(b, g),
                      asking, asking if quarter == G - 1 else None,
                      after(2 if own_q else 0, of_group(maxima, n + MAX)),
                      after(2, of_group(max_rows_of, n + ROWS)),
                      finish(*seq[n - 1]) if n else None,
                      norm_quarter(n + QUERY) if own_q and n + QUERY < last else None,
                      *side)
                if g == 0 and b + 1 < B:
                    load_values(b + 1)
                if g == 0 and b > 0:
                    load_base(b - 1)
            while late:
                values(*late.pop(0))
            while pair_sums:
                sum_pair(*pair_sums.pop(0))
            load_base(B - 1)
            weave(finish(*seq[-1]))
            add_base(B - 1)
            weave(project(B - 1))
            block()

    attention_stage("L0", a["x"], x1, "L0_bq", a["L0_xcond_Wp"], a["L0_xcond_bp"], 0, "qkv")

    with ExitStack() as ctx:
        stage_name[0] = "qkv"
        AHEAD = 2
        wide = Ring([sb(ctx, f"wide{i}", [P, N]) for i in range(2)])
        parts = Ring([(sb(ctx, f"x_hi{i}", [P, KC, N], F32R), sb(ctx, f"x_lo{i}", [P, KC, N], F32R)) for i in range(2)])
        proj = Ring(range(8))
        start = starts["qkv"]
        norm = start.norm
        norm.into(wide, proj, parts)
        o_parts = Ring([sb(ctx, f"qk_parts{i}", [P, 2, N], F32R) for i in range(3)])
        v_rows = Ring([sb(ctx, f"value_rows{i}", [P, D]) for i in range(3)])
        bias_tile = sb(ctx, "value_bias_tile", [P, D])
        w_qkv = Weights(ctx, "w_qkv", a["L1_xcond_W_qkv"])
        w_hi, w_lo = w_qkv.hi, w_qkv.lo
        batch = [start.batch0] + [{} for _ in range(B - 1)]
        start.stream.split(w_qkv)
        weave(start.turning, after(2, (start.stream.split(w_qkv) for _ in range(AHEAD - 1))))
        t_bias = load("value_bias", bias_tile[:], a["L1_xcond_b_qkv"][2 * D:3 * D].partition_broadcast(P))
        for b in range(B):
            xh, xl = batch[b]["xh"], batch[b]["xl"]
            turning = norm.batch(b + 1, batch[b + 1]) if b + 1 < B else iter(())
            pe.wait(*batch[b]["t_parts"])
            for m in range(2 * G):
                if b == 0:
                    start.stream.split(w_qkv)
                    if m >= 2 * G - 2:
                        start.stream.split(w_qkv)
                pe.wait(*w_qkv.ready[m])
                pi, bk = proj.take(pe)
                f = slice(m * P, (m + 1) * P)
                tp = product(bank[:, bk, :], [(w_hi[:, c, f], w_lo[:, c, f], xh[:, c, :], xl[:, c, :]) for c in range(KC)])
                oi, ot = o_parts.take(act, dve)
                col = bias_col["L1_b_qkv"] + m
                th, tl = parts_of(bank[:, bk, :], wide, ot[:, 0, :], ot[:, 1, :], (tp,), bias=bias_cols[:, col:col + 1])
                proj.free(pi, th)
                sp.wait(th, tl)
                dst = q_parts["self"] if m < G else k_self
                o_parts.free(oi, store_parts(f"qk_store{oi}", dst[b, m % G], ot))
                for _ in range({0: 1, 2: 2, 3: 2, 4: 1, 5: 2, 6: 2, 7: 1}.get(m, 0)):
                    next(turning, None)
            pe.wait(*(t for m in range(2 * G, 3 * G) for t in w_qkv.ready[m]))
            for t in range(NT):
                pi, bk = proj.take(pe)
                r = slice(t * P, (t + 1) * P)
                tp = product(bank[:, bk, :], [(xh[:, c, r], xl[:, c, r], w_hi[:, c, 2 * D:3 * D], w_lo[:, c, 2 * D:3 * D])
                                              for c in range(KC)])
                vi, vt = v_rows.take(dve)
                dve.wait(tp, t_bias)
                tv = dve.do(lambda e, bk=bk, vt=vt: e.tensor_tensor(vt[:], bank[:, bk, :], bias_tile[:], ALU.add), c_res)
                proj.free(pi, tv)
                sp.wait(tv)
                v_rows.free(vi, load(f"value_store{vi}", v_self[b, r, :], vt[:]))
                next(turning, None)
            parts.free(batch[b]["parts_i"], tp)
            weave(turning)
        block()

    attention_stage("self", x1, x2, None, a["L1_xcond_W_proj"], None, None, "cross")
    attention_stage("cross", x2, x3, "L1_b_qc", a["L1_xcond_W_cproj"], a["L1_xcond_b_cproj"], 1, "mlp")

    with ExitStack() as ctx:
        stage_name[0] = "mlp"
        LAG = 2
        x_rows = sb(ctx, "x_rows", [P, NT, D])
        wide = Ring([sb(ctx, f"wide{i}", [P, N]) for i in range(2)])
        parts = Ring([(sb(ctx, f"x_hi{i}", [P, KC, N], F32R), sb(ctx, f"x_lo{i}", [P, KC, N], F32R)) for i in range(2)])
        acc = [4, 5, 6, 7]
        up = Ring(range(4))
        start = starts["mlp"]
        norm = start.norm
        norm.into(wide, up, parts)
        h_parts = Ring([sb(ctx, f"hidden_parts{i}", [P, 2, N], F32R) for i in range(LAG + 1)])
        gt = sb(ctx, "gate_and_bias", [P, 2, D])
        w1, w2 = Weights(ctx, "w_mlp1", w_up), Weights(ctx, "w_mlp2", w_down)
        acc_free = [()] * NT
        rows_free = ()
        batch = [start.batch0] + [{} for _ in range(B - 1)]
        start.stream.split(w1)
        weave(start.turning, after(2, (start.stream.split(w1) for _ in range(UP_AHEAD - 1))))

        def down(j, hi_, ht, ticks):
            pe.wait(*ticks, *w2.ready[j])
            tiles = []
            for t in range(NT):
                if j == 0:
                    pe.wait(*acc_free[t])
                r = slice(t * P, (t + 1) * P)
                terms = [(ht[:, 0, r], w2.hi[:, j, :]), (ht[:, 0, r], w2.lo[:, j, :]), (ht[:, 1, r], w2.hi[:, j, :])]
                for k, (l, w) in enumerate(terms):
                    tick = pe.do(lambda e, l=l, w=w, k=k, t=t: e.matmul(
                        bank[:, acc[t], :], l, w, start=j == 0 and k == 0, stop=j == JC - 1 and k == 2), c_proj)
                tiles.append(tick)
            h_parts.free(hi_, tick)
            return tiles

        for b in range(B):
            xh, xl = batch[b]["xh"], batch[b]["xl"]
            turning = norm.batch(b + 1, batch[b + 1]) if b + 1 < B else iter(())
            next(turning, None)
            sp.wait(*rows_free)
            t_x = load("x_rows", x_rows[:], x3[b].rearrange("(t p) d -> p t d", p=P))
            for w in range(2):
                t_g = load("mlp_gate", gt[:, w, :], gate_rows[1, w, b].partition_broadcast(P))
            pe.wait(*batch[b]["t_parts"])
            pending = []
            for j in range(JC):
                if b == 0:
                    start.stream.split(w2)
                    if j + UP_AHEAD < JC:
                        start.stream.split(w1)
                pe.wait(*w1.ready[j])
                ui, bk = up.take(pe)
                f = slice(j * P, (j + 1) * P)
                tp = product(bank[:, bk, :], [(w1.hi[:, c, f], w1.lo[:, c, f], xh[:, c, :], xl[:, c, :]) for c in range(KC)])
                wi, w = wide.take(act)
                hi_, ht = h_parts.take(act, dve)
                act.wait(tp)
                col = bias_col["L1_b_mlp1"] + j
                tw = act.do(lambda e, w=w, bk=bk, col=col: e.activation(w[:], bank[:, bk, :], ACT.Gelu_apprx_tanh,
                                                               bias=bias_cols[:, col:col + 1]), c_wide)
                up.free(ui, tw)
                act.wait(tw)
                th = act.do(lambda e, w=w, ht=ht: e.copy(ht[:, 0, :], w[:]), c_hi)
                dve.wait(th)
                tl = dve.do(lambda e, w=w, ht=ht: e.tensor_tensor(ht[:, 1, :], w[:], raw(ht[:, 0, :]), ALU.subtract), c_lo)
                wide.free(wi, tl)
                pending.append((j, hi_, ht, (th, tl)))
                if len(pending) == LAG:
                    down(*pending.pop(0))
                if j > 0 and j != 6:
                    next(turning, None)
                if j == 8:
                    pool.wait(t_x, t_g)
                    for t in range(NT):
                        t_base = pool.do(lambda e, t=t: e.tensor_tensor(
                            x_rows[:, t, :], x_rows[:, t, :], gt[:, 1, :], ALU.add), c_xb)
            parts.free(batch[b]["parts_i"], tp)
            weave(turning)
            for item in pending:
                tiles = down(*item)
            for t in range(NT):
                pi, pr = wide.take(dve)
                dve.wait(tiles[t], t_g, t_base)
                tg = dve.do(lambda e, t=t, pr=pr: e.tensor_tensor(pr[:], bank[:, acc[t], :], gt[:, 0, :], ALU.mult), c_res)
                acc_free[t] = (tg,)
                dve.wait(tg)
                tres = dve.do(lambda e, t=t, pr=pr: e.tensor_tensor(x_rows[:, t, :], pr[:], x_rows[:, t, :], ALU.add), c_res)
                wide.free(pi, tres)
            sp.wait(tres)
            rows_free = (load("x_out", out[b].rearrange("(t p) d -> p t d", p=P), x_rows[:]),)
        block()


_INS = ["x", "ctx_1024", "cond_1024"] + ["L0_xcond_" + n for n in (
    "Wq", "bq", "Wkv", "bkv", "Wp", "bp", "Wss_q", "bss_q", "Wss_kv", "bss_kv")] + ["L1_xcond_" + n for n in (
    "W_mod", "b_mod", "W_qkv", "b_qkv", "W_proj", "b_proj", "W_qc", "b_qc", "W_kvc", "b_kvc", "W_cproj", "b_cproj",
    "W_mlp1", "b_mlp1", "W_mlp2", "b_mlp2")]


def kernel(**inputs):
    import numpy as _np
    import concourse.bacc as _bacc
    from concourse import mybir as _mybir
    from concourse.bass_utils import run_bass_kernel_spmd as _run

    nc = _bacc.Bacc("TRN2", target_bir_lowering=False, num_devices=1)
    arrays, args = {}, {}
    for name in _INS:
        v = _np.ascontiguousarray(inputs[name])
        arrays[f"in_{name}"] = v
        args[name] = nc.dram_tensor(f"in_{name}", v.shape, _mybir.dt.from_np(v.dtype), kind="ExternalInput").ap()
    out = nc.dram_tensor("out", (B, N, D), F32, kind="ExternalOutput").ap()
    build(nc, args, out)
    r = _run(nc, [arrays], core_ids=[0])
    return r.results[0]["out"]
```
